# Optimizing a Trainium2 kernel written in Bass

```python
import numpy as np
import jax
import jax.numpy as jnp

def _softmax(x, axis=-1):
    return jax.nn.softmax(x, axis=axis)

def _gelu(x):
    return jax.nn.gelu(x, approximate=True)

def _silu(x):
    return jax.nn.silu(x)

def _sigmoid(x):
    return jax.nn.sigmoid(x)

def _layernorm(x, axis=-1, eps=1e-05):
    m = jnp.mean(x, axis=axis, keepdims=True)
    v = jnp.var(x, axis=axis, keepdims=True)
    return (x - m) / jnp.sqrt(v + eps)

def _scatter_add(tgt, idx, src, axis=0):
    return tgt.at[idx].add(src)

def _segment_sum(src, seg, n):
    return jax.ops.segment_sum(src, seg, n)
kernel_name = 'mk_adj_resnorm_d4_adj_r2_7f3ae9'

def setup_inputs(seed: int=0):
    np.random.seed(seed)
    _w = jnp.asarray

    def _rec_inputs():
        import jax
        import jax.numpy as jnp
        _gk = jax.random.key(seed)
        x = -0.0001071 + 1.001 * jax.random.normal(jax.random.fold_in(_gk, 1), (8, 1500, 64), jnp.float32)
        _a = jax.random.bernoulli(jax.random.fold_in(_gk, 2), 0.00266667, (8, 1500, 1500))
        _a = jnp.logical_or(_a, jnp.swapaxes(_a, -1, -2))
        _a = jnp.logical_or(_a, jnp.eye(1500, dtype=bool))
        _af = _a.astype(jnp.float32)
        adj = _af
        return (x, adj)
    x, adj = _rec_inputs()

    def _L0_gnn_setup():
        import jax, jax.numpy as jnp
        import numpy as np
        B, N, F = (2, 1500, 64)
        H, OUT, ATT = (4, 16, 16)
        DENSITY = 0.01
        key = jax.random.key(seed)
        ks = jax.random.split(key, 6)
        h = jax.random.normal(ks[0], (B, N, F), dtype=jnp.float32)
        a = (jax.random.uniform(ks[1], (B, N, N)) < DENSITY).astype(jnp.float32)
        glorot = lambda k, shape: jax.random.uniform(k, shape, jnp.float32, -1.0, 1.0) * jnp.sqrt(6.0 / (shape[-2] + shape[-1]))
        kernel = glorot(ks[2], (H, F, OUT))
        attention_kernel = glorot(ks[3], (H, F, ATT))
        attention_kernel_2 = glorot(ks[4], (H, F, ATT))
        bias = jax.random.normal(ks[5], (1, 1, H, OUT), dtype=jnp.float32) * 0.01
        return {'h': h, 'a': a, 'kernel': kernel, 'attention_kernel': attention_kernel, 'attention_kernel_2': attention_kernel_2, 'bias': bias}
    _L0_gnn_all = _L0_gnn_setup()
    _L0_gnn_in = {k: v for k, v in _L0_gnn_all.items() if k in ('kernel', 'attention_kernel', 'attention_kernel_2', 'bias')}
    del _L0_gnn_all

    def _L1_gnn_setup():
        import jax, jax.numpy as jnp
        import numpy as np
        key = jax.random.key(seed)
        k1, k2 = jax.random.split(key)
        B, N, D = (16, 1024, 64)
        nodes = jax.random.normal(k1, (B, N, D), dtype=jnp.float32)
        edges = jax.random.uniform(k2, (B, N, N), dtype=jnp.float32)
        return {'nodes': nodes, 'edges': edges}
    _L1_gnn_all = _L1_gnn_setup()
    _L1_gnn_in = {k: v for k, v in _L1_gnn_all.items() if k in ()}
    del _L1_gnn_all

    def _L2_gnn_setup():
        import jax, jax.numpy as jnp
        import numpy as np
        B, L, F = (8, 2048, 64)
        key = jax.random.key(seed)
        k1, k2, k3, k4 = jax.random.split(key, 4)
        text = jax.random.normal(k1, (B, L, F), dtype=jnp.float32)
        adj = jax.random.uniform(k2, (B, L, L), dtype=jnp.float32)
        weight = jax.random.normal(k3, (F, F), dtype=jnp.float32) * (1.0 / np.sqrt(F))
        bias = jax.random.normal(k4, (F,), dtype=jnp.float32) * 0.01
        return {'text': text, 'adj': adj, 'weight': weight, 'bias': bias}
    _L2_gnn_all = _L2_gnn_setup()
    _L2_gnn_in = {k: v for k, v in _L2_gnn_all.items() if k in ('weight', 'bias')}
    del _L2_gnn_all

    def _L3_gnn_setup():
        import jax, jax.numpy as jnp
        import numpy as np
        key = jax.random.key(seed)
        kx, ka = jax.random.split(key)
        B, N, F = (8, 1024, 64)
        x = jax.random.normal(kx, (B, N, F), dtype=jnp.float32)
        a = jax.random.uniform(ka, (B, N, N), dtype=jnp.float32)
        return {'x': x, 'a': a}
    _L3_gnn_all = _L3_gnn_setup()
    _L3_gnn_in = {k: v for k, v in _L3_gnn_all.items() if k in ()}
    del _L3_gnn_all
    return {'x': x, 'adj': adj, 'L0_gnn_kernel': _L0_gnn_in['kernel'], 'L0_gnn_attention_kernel': _L0_gnn_in['attention_kernel'], 'L0_gnn_attention_kernel_2': _L0_gnn_in['attention_kernel_2'], 'L0_gnn_bias': _L0_gnn_in['bias'], 'L2_gnn_weight': _L2_gnn_in['weight'], 'L2_gnn_bias': _L2_gnn_in['bias']}

def reference(x, adj, L0_gnn_kernel, L0_gnn_attention_kernel, L0_gnn_attention_kernel_2, L0_gnn_bias, L2_gnn_weight, L2_gnn_bias):
    import jax
    import jax.numpy as jnp

    def _L0_gnn_ref(h, a, kernel, attention_kernel, attention_kernel_2, bias):
        import jax, jax.numpy as jnp
        import numpy as np
        B, N, F = (2, 1500, 64)
        H, OUT, ATT = (4, 16, 16)
        DENSITY = 0.01
        feats = jnp.einsum('bnf,hfo->bhno', h, kernel)
        f_self = jnp.einsum('bnf,hfd->hbnd', h, attention_kernel)
        f_other = jnp.einsum('bnf,hfd->hbdn', h, attention_kernel_2)
        a_h = a[None]
        scores = jnp.einsum('hbnd,hbdm->hbnm', f_self, f_other)
        masked = a_h * scores
        masked = jnp.where(masked >= 0, masked, 0.2 * masked)
        masked = masked / jnp.sqrt(jnp.float32(ATT))
        masked = masked + jnp.where(a_h == 0, jnp.float32(-1000000000.0), jnp.float32(0.0))
        attn = jax.nn.softmax(masked, axis=-1)
        attn = attn * jnp.where(a_h == 0, jnp.float32(0.0), jnp.float32(1.0))
        attn = jnp.transpose(attn, (1, 0, 2, 3))
        node_features = jnp.einsum('bhnm,bhmo->bhno', attn, feats)
        node_features = node_features + jnp.transpose(bias, (0, 2, 1, 3))
        node_features = jax.nn.relu(node_features)
        node_features = jnp.transpose(node_features, (0, 2, 1, 3))
        return node_features.reshape(-1, N, H * OUT)

    def _L1_gnn_ref(nodes, edges):
        import jax, jax.numpy as jnp
        import numpy as np
        N = nodes.shape[1]
        A = edges + jnp.eye(N, dtype=edges.dtype)
        num = jnp.einsum('bij,bjd->bid', A, nodes)
        denom = jnp.sum(A, axis=2, keepdims=True)
        out = num / denom
        return jnp.where(jnp.isnan(out), jnp.zeros_like(out), out)

    def _L2_gnn_ref(text, adj, weight, bias):
        import jax, jax.numpy as jnp
        import numpy as np
        B, L, F = (8, 2048, 64)
        hidden = jnp.einsum('blf,fo->blo', text, weight)
        out = jnp.einsum('bij,bjo->bio', adj, hidden)
        return out + bias

    def _L3_gnn_ref(x, a):
        import jax, jax.numpy as jnp
        import numpy as np
        t = jnp.einsum('bij,bjf->bif', a, x)
        out = jnp.where(t > 0.5, t / t, t * 0.0)
        return out
    x = _layernorm(x + _L0_gnn_ref(x, adj, L0_gnn_kernel, L0_gnn_attention_kernel, L0_gnn_attention_kernel_2, L0_gnn_bias), axis=-1)
    x = _layernorm(x + _L1_gnn_ref(x, adj), axis=-1)
    x = _layernorm(x + _L2_gnn_ref(x, adj, L2_gnn_weight, L2_gnn_bias), axis=-1)
    x = _layernorm(x + _L3_gnn_ref(x, adj), axis=-1)
    return x

_drawn_inputs = setup_inputs


def setup_inputs(seed=0):
    import zlib

    import numpy as np

    out = dict(_drawn_inputs(seed))
    spreads = {}
    factors = {}
    for name, (base, spread) in spreads.items():
        noise = np.random.default_rng([zlib.crc32(name.encode()), seed]).standard_normal(out[name].shape)
        drawn = base * np.exp(spread * noise) if base else spread * noise
        out[name] = jnp.asarray(drawn.astype(out[name].dtype))
    for name, factor in factors.items():
        out[name] = (out[name] * factor).astype(out[name].dtype)
    return out
```

```python
import concourse.bass as bass
from concourse import mybir
from contextlib import ExitStack

B, N, F = 8, 1500, 64
H, D = 4, 16
P = 125
NT = N // P
ST = 4
NS = NT // ST
C = ST * P
NG = B * NS
TPS = H * ST
VW = 32
TERMS = [(0, 0), (0, 1), (0, 2), (1, 0), (1, 1), (2, 0)]
KS = len(TERMS) * D
BIG = 2.0 ** 30
FLOOR = -1.0e6
EPS = 1e-5


def adj_resnorm(nc, x, adj, wv, wself, wother, bias0, w2, bias2, out):
    f32, bf16, f16, f8 = mybir.dt.float32, mybir.dt.bfloat16, mybir.dt.float16, mybir.dt.float8e4
    ALU, ACT, AX = mybir.AluOpType, mybir.ActivationFunctionType, mybir.AxisListType

    x_v = x.rearrange("b (s i k) f -> b i s k f", i=P, k=ST)
    out_v = out.rearrange("b (s i k) f -> b i s k f", i=P, k=ST)
    adj_v = adj.rearrange("b n m -> (b n) m").rearrange("(g i k) m -> g k i m", i=P, k=ST)

    ctx = ExitStack()
    with ctx:
        def sb(name, shape, dt):
            return ctx.enter_context(nc.sbuf_tensor(name, shape, dt))

        def sem(name):
            return ctx.enter_context(nc.semaphore(name))

        A = sb("A", [P, ST, N], bf16)
        A8 = sb("A8", [P, ST, N], f8)
        NEG = sb("NEG", [P, ST, N], bf16)
        AT = sb("AT", [P, NS, N, ST], f8)
        FS = sb("FS", [KS, H, N], bf16)
        FO = sb("FO", [KS, H, N], bf16)
        R = sb("R", [P, 4, N], f32)
        L = sb("L", [P, 4, N], f32)
        PT = sb("PT", [P, 2, NT, C], f32)
        V = sb("V", [P, NT, H, VW], f32)
        XT = sb("XT", [F, N], f32)
        PARTS = sb("PARTS", [128, 3, N], bf16)
        REST = sb("REST", [128, N], f32)
        O4 = sb("O4", [128, C], f32)
        OS = sb("OS", [P, NT, H, D + 1], f32)
        X = sb("X", [P, NT, F], f32)
        Y = sb("Y", [P, NT, F], f32)
        XP = sb("XP", [P, NT, 2 * F], f16)
        YT = REST
        RDEN = sb("RDEN", [P, NT], f32)
        RSUM = sb("RSUM", [P, NT, H], f32)
        MEAN = sb("MEAN", [P, NT], f32)
        RSTD = sb("RSTD", [P, NT], f32)
        CMAX = sb("CMAX", [P, 4, 3], f32)
        RMAX = sb("RMAX", [P, 4], f32)
        SHIFT = sb("SHIFT", [P, 4], f32)
        WV = sb("WV", [F, H, D], f32)
        WA = sb("WA", [F, 2, H, D], f32)
        WW = sb("WW", [128, 2, F], f32)
        B0 = sb("B0", [P, F], f32)
        B2 = sb("B2", [P, F], f32)
        ID = sb("ID", [128, 128], f32)
        E4 = sb("E4", [128, VW], f32)
        ONES = sb("ONES", [P, 1], bf16)
        NHALF = sb("NHALF", [P, NT], f32)

        SP_ = ctx.enter_context(nc.psum_tensor("SP_", [128, 3, 512], f32))
        TP = ctx.enter_context(nc.psum_tensor("TP", [128, 3, 512], f32))
        M0 = ctx.enter_context(nc.psum_tensor("M0", [128, 512], f32))
        M1 = ctx.enter_context(nc.psum_tensor("M1", [128, 512], f32))

        weights_in = sem("weights_in")
        const_ok = sem("const_ok")
        x_in = sem("x_in")
        a_in = [sem(f"a_in{k}") for k in range(ST)]
        stood = {e: sem(f"stood_{e}") for e in ("pe", "dve", "pool")}
        neg_ready = sem("neg_ready")
        a8_ready = sem("a8_ready")
        xt_psum, xt_ready, f_psum, hi_ready, rest_ready, mid_ready, lo_ready, v_ready, split_in = [
            sem(n) for n in ("xt_psum", "xt_ready", "f_psum", "hi_ready", "rest_ready", "mid_ready", "lo_ready",
                             "v_ready", "split_in")]
        scores = sem("scores")
        relus = sem("relus")
        bank_free = sem("bank_free")
        rmax_ok = sem("rmax_ok")
        shift_ok = sem("shift_ok")
        l_ready = sem("l_ready")
        turned = sem("turned")
        exps = sem("exps")
        pv_done = sem("pv_done")
        o4_ready = sem("o4_ready")
        m1_filled = sem("m1_filled")
        m1_read = sem("m1_read")
        deg_psum = sem("deg_psum")
        parts_ready = sem("parts_ready")
        xh_ready = sem("xh_ready")
        x_ready = sem("x_ready")
        var_ok = sem("var_ok")
        rstd_ok = sem("rstd_ok")
        yt_psum = sem("yt_psum")
        yt_ready = sem("yt_ready")
        y_psum = sem("y_psum")
        dve_seq = sem("dve_seq")
        stored = sem("stored")
        block = ctx.enter_context(nc.Block())

        NSPLIT = 2 * len(TERMS) * H

        @block.sync
        def _(sp):
            sp.sem_inc(stored, 16)
            sp.dma_start(WV[:, :, :], wv.rearrange("h f o -> f h o")).then_inc(weights_in, 16)
            sp.dma_start(WA[:, 0, :, :], wself.rearrange("h f o -> f h o")).then_inc(weights_in, 16)
            sp.dma_start(WA[:, 1, :, :], wother.rearrange("h f o -> f h o")).then_inc(weights_in, 16)
            sp.dma_start(WW[0:F, 1, :], w2).then_inc(weights_in, 16)
            sp.dma_start(WW[F:2 * F, 1, :], w2).then_inc(weights_in, 16)
            sp.dma_start(B0[:, :], bias0.rearrange("a b h o -> (a b h o)").partition_broadcast(P)).then_inc(weights_in, 16)
            sp.dma_start(B2[:, :], bias2.partition_broadcast(P)).then_inc(weights_in, 16)
            with sp.Fori(0, B) as b:
                sp.wait_ge(stored, b * 16 + 16)
                sp.dma_start(X[:, :, :].rearrange("p (s k) f -> p s k f", k=ST), x_v[b]).then_inc(x_in, 16)
                sp.wait_ge(hi_ready, b + 1)
                sp.wait_ge(mid_ready, b + 1)
                sp.wait_ge(lo_ready, b + 1)
                for g, pair in enumerate(TERMS):
                    for side, dst in enumerate((FS, FO)):
                        for h in range(H):
                            sp.dma_start(dst[g * D:(g + 1) * D, h, :],
                                         PARTS[side * F + h * D:side * F + (h + 1) * D, pair[side], :]).then_inc(split_in, 16)
                sp.wait_ge(x_ready, b * 4 + 4)
                sp.dma_start(out_v[b], X[:, :, :].rearrange("p (s k) f -> p s k f", k=ST)).then_inc(stored, 16)
            sp.wait_ge(stored, 16 * B + 16)

        @block.gpsimd
        def _(pool):
            nc.gpsimd.memset(ID[:, :], 0.0).then_inc(const_ok, 1)
            nc.gpsimd.memset(E4[:, :], 0.0).then_inc(const_ok, 1)
            nc.gpsimd.memset(WW[:, 0, :], 0.0).then_inc(const_ok, 1)
            nc.gpsimd.memset(ONES[:, :], 1.0).then_inc(const_ok, 1)
            nc.gpsimd.memset(V[:, :, :, D:VW], 0.0).then_inc(const_ok, 1)
            nc.gpsimd.memset(NHALF[:, :], -0.5).then_inc(const_ok, 1)
            pool.wait_ge(const_ok, 6)
            nc.gpsimd.memset(V[:, :, :, D:D + 1], 1.0).then_inc(const_ok, 1)
            n = 7
            nc.gpsimd.affine_select(out=ID[:, :], in_=ID[:, :], compare_op=ALU.not_equal, fill=1.0, base=0,
                                    pattern=[[-1, 128]], channel_multiplier=1).then_inc(const_ok, 1)
            n += 1
            for c in range(4):
                nc.gpsimd.affine_select(out=E4[:, :], in_=E4[:, :], compare_op=ALU.not_equal, fill=1.0,
                                        base=-VW * c, pattern=[[-1, VW]], channel_multiplier=1).then_inc(const_ok, 1)
                n += 1
                pool.wait_ge(const_ok, n)
            for c in range(2):
                nc.gpsimd.affine_select(out=WW[:, 0, :], in_=WW[:, 0, :], compare_op=ALU.not_equal, fill=1.0,
                                        base=-F * c, pattern=[[-1, F]], channel_multiplier=1).then_inc(const_ok, 1)
                n += 1
                pool.wait_ge(const_ok, n)
            assert n == 14

            def load(g, k):
                pool.dma_start(A[:, k, :], adj_v[g, k]).then_inc(a_in[k], 16)

            def negate(k):
                nc.gpsimd.tensor_scalar(NEG[:, k, :].rearrange("p (s k i) -> p s i k", k=ST, i=P),
                                        A[:, k, :].rearrange("p (s i k) -> p s i k", i=P, k=ST),
                                        -1.0, BIG, ALU.add, ALU.mult).then_inc(neg_ready, 1)

            def narrow(k):
                nc.gpsimd.tensor_copy(A8[:, k, :], A[:, k, :], saturate=False).then_inc(a8_ready, 1)

            for k in range(ST):
                load(0, k)
            for k in range(ST):
                pool.wait_ge(a_in[k], 16)
                narrow(k)
                negate(k)

            def refill(g):
                for k in range(ST):
                    pool.wait_ge(neg_ready, g * ST + k + 1)
                    pool.wait_ge(a8_ready, g * ST + k + 1)
                    load(g + 1, k)
                for k in range(ST):
                    pool.wait_ge(m1_read, g * 8 + (0, 1, 3, 5)[k] + 1 + 1)
                    pool.wait_ge(a_in[k], g * 16 + 32).then_inc(stood["pool"], 1)
                    narrow(k)
                for k in range(ST):
                    pool.wait_ge(bank_free, g * (3 * TPS) + 3 * (TPS - ST + k) + 3 + 3).then_inc(stood["pool"], 1)
                    negate(k)

            def rstd(b):
                for l in range(4):
                    pool.wait_ge(var_ok, b * 4 + l + 1)
                    nc.gpsimd.tensor_tensor(RSTD[:, :], RSTD[:, :], NHALF[:, :], ALU.pow).then_inc(rstd_ok, 1)

            with pool.Fori(0, B - 1) as b:
                with pool.Fori(0, NS) as s:
                    refill(b * NS + s)
                rstd(b)
            with pool.Fori(0, NS - 1) as s:
                refill(s + (B - 1) * NS)
            rstd(B - 1)

        @block.tensor
        def _(pe):
            pe.wait_ge(weights_in, 7 * 16)
            pe.wait_ge(const_ok, 14)
            with pe.Fori(0, B) as b:
                pe.wait_ge(x_in, b * 16 + 16).then_inc(stood["pe"], 1)
                for t in range(NT):
                    last = nc.tensor.transpose(TP[:F, t // 4, (t % 4) * P:(t % 4 + 1) * P], X[:, t, :], ID[:P, :P])
                last.then_inc(xt_psum, 1)
                pe.wait_ge(xt_ready, b + 1)
                for t in range(NT):
                    nc.tensor.matmul(SP_[:P, t // 8, (t % 8) * F:(t % 8 + 1) * F], XT[:, t * P:(t + 1) * P],
                                     WV[:, :, :].rearrange("f h o -> f (h o)"), start=True, stop=True)
                for c in range(3):
                    last = nc.tensor.matmul(TP[:, c, 0:C], WA[:, :, :, :].rearrange("f s h o -> f (s h o)"),
                                            XT[:, c * C:(c + 1) * C], start=True, stop=True)
                last.then_inc(f_psum, 1)
                pe.wait_ge(v_ready, b + 1).then_inc(stood["pe"], 1)
                pe.wait_ge(split_in, b * (16 * NSPLIT) + 16 * NSPLIT).then_inc(stood["pe"], 1)

                with pe.Fori(0, NS) as s:
                    g = b * NS + s

                    def score(j):
                        h, k = divmod(j, ST)
                        for c in range(3):
                            pe.wait_ge(bank_free, g * (3 * TPS) + 3 * j + c + 1)
                            nc.tensor.matmul(SP_[:P, c, 0:C], FS[:, h, bass.ds(s * C + k * P, P)],
                                             FO[:, h, c * C:(c + 1) * C], start=True, stop=True).then_inc(scores, 1)

                    def turn(j):
                        pe.wait_ge(l_ready, g * TPS + j + 1 + 4)
                        pe.wait_ge(exps, g * TPS + j + 1)
                        for m in range(NT):
                            last = nc.tensor.transpose(TP[:P, m // 4, (m % 4) * P:(m % 4 + 1) * P],
                                                       L[:, j % 4, m * P:(m + 1) * P], ID[:P, :P])
                        last.then_inc(turned, 1)

                    def weigh(h):
                        pe.wait_ge(exps, g * TPS + 4 * h + 4 + 1)
                        pe.wait_ge(o4_ready, g * H + h + 1)
                        for r in range(3):
                            for c in range(4):
                                last = nc.tensor.matmul(M0[VW * c:VW * (c + 1), 0:C], V[:, 3 * c + r, h, :],
                                                        PT[:, h % 2, 3 * c + r, :], start=(r == 0), stop=(r == 2))
                        last.then_inc(pv_done, 1)

                    def gather(h, n):
                        pe.wait_ge(o4_ready, g * H + h + 1 + 1)
                        pe.wait_ge(m1_read, g * 8 + n + 1)
                        for k in range(ST):
                            last = nc.tensor.matmul(M1[:P, k * VW:k * VW + D + 1], O4[:, k * P:(k + 1) * P],
                                                    E4[:, 0:D + 1], start=True, stop=True)
                        last.then_inc(m1_filled, 1)

                    def turn_adj(k, n):
                        pe.wait_ge(a8_ready, g * ST + k + 1)
                        pe.wait_ge(m1_read, g * 8 + n + 1)
                        words = A8[:, k, :].bitcast(f32)
                        for q in range(NS):
                            last = nc.tensor.transpose(M1[:P, q * P:(q + 1) * P], words[:, q * P:(q + 1) * P], ID[:P, :P])
                        last.then_inc(m1_filled, 1)

                    score(0)
                    score(1)
                    for j in range(TPS):
                        h, k = divmod(j, ST)
                        if j + 2 < TPS:
                            score(j + 2)
                        turn(j)
                        if k == 0:
                            turn_adj(h, (0, 1, 3, 5)[h])
                        if k == 0 and h:
                            weigh(h - 1)
                        if k == 2 and h:
                            gather(h - 1, (2, 4, 6)[h - 1])
                    weigh(H - 1)
                    gather(H - 1, 7)

                pe.wait_ge(m1_read, b * (8 * NS) + 8 * NS + 1).then_inc(stood["pe"], 1)
                for t in range(NT):
                    for m in range(NT):
                        last = nc.tensor.matmul(M1[:P, t:t + 1], AT[:, m // ST, t * P:(t + 1) * P, m % ST],
                                                ONES[:, :], start=(m == 0), stop=(m == NT - 1))
                last.then_inc(deg_psum, 1)
                for l in range(3):
                    pe.wait_ge(parts_ready, b * 3 + l + 1).then_inc(stood["pe"], 1)
                    for c in range(3):
                        for m in range(NT):
                            last = nc.tensor.matmul(SP_[:, c, 0:C], XP[:, m, :],
                                                    AT[:, m // ST, c * C:(c + 1) * C, m % ST],
                                                    start=(m == 0), stop=(m == NT - 1))
                    last.then_inc(yt_psum, 1)
                    pe.wait_ge(yt_ready, b * 3 + l + 1)
                    for t in range(NT):
                        last = nc.tensor.matmul(TP[:P, t // 8, (t % 8) * F:(t % 8 + 1) * F], YT[:, t * P:(t + 1) * P],
                                                WW[:, 1 if l == 1 else 0, :], start=True, stop=True)
                    last.then_inc(y_psum, 1)

        @block.scalar
        def _(act):
            with act.Fori(0, B) as b:
                act.wait_ge(xt_psum, b + 1)
                nc.scalar.activation(XT[:, :].rearrange("p (a c) -> p a c", a=3), TP[:F, :, 0:C], ACT.Copy).then_inc(xt_ready, 1)
                act.wait_ge(f_psum, b + 1)
                nc.scalar.activation(PARTS[:, 0, :].rearrange("p (a c) -> p a c", a=3), TP[:, :, 0:C], ACT.Copy).then_inc(hi_ready, 1)
                act.wait_ge(rest_ready, b + 1)
                nc.scalar.activation(PARTS[:, 1, :], REST[:, :], ACT.Copy).then_inc(mid_ready, 1)
                with act.Fori(0, NS) as s:
                    g = b * NS + s

                    def relu(j):
                        act.wait_ge(l_ready, g * TPS + j + 1)
                        for c in range(3):
                            act.wait_ge(scores, g * (3 * TPS) + 3 * j + c + 1)
                            nc.scalar.activation(R[:, j % 4, c * C:(c + 1) * C], SP_[:P, c, 0:C], ACT.Relu,
                                                 scale=4.0).then_inc(relus, 1)

                    def expo(j):
                        h, k = divmod(j, ST)
                        act.wait_ge(turned, g * TPS + j + 1 + 4)
                        nc.scalar.activation(PT[:, h % 2, :, k * P:(k + 1) * P].rearrange("p (a m) n -> p a m n", a=3),
                                             TP[:P, :, 0:C].rearrange("p a (m n) -> p a m n", m=4), ACT.Exp,
                                             scale=0.05).then_inc(exps, 1)

                    def take(h):
                        act.wait_ge(pv_done, g * H + h + 1)
                        if h == 0:
                            act.wait_ge(m1_filled, g * 8 + 1)
                        else:
                            act.wait_ge(m1_filled, g * 8 + (0, 3, 5, 7)[h] + 1)
                        nc.scalar.activation(O4[:, :], M0[:, 0:C], ACT.Copy).then_inc(o4_ready, 1)

                    relu(0)
                    relu(1)
                    for j in range(TPS):
                        if j + 2 < TPS:
                            relu(j + 2)
                        expo(j)
                        if j % ST == 1 and j > ST:
                            take(j // ST - 1)
                    take(H - 1)
                act.wait_ge(m1_filled, b * (8 * NS) + 8 * NS + 1)
                for l in range(3):
                    act.wait_ge(x_ready, b * 4 + l + 1)
                    nc.scalar.activation(XP[:, :, 0:F], X[:, :, :], ACT.Copy).then_inc(xh_ready, 1)
                    act.wait_ge(yt_psum, b * 3 + l + 1)
                    nc.scalar.activation(YT[:, :].rearrange("p (a c) -> p a c", a=3), SP_[:, :, 0:C], ACT.Copy).then_inc(yt_ready, 1)

        LINKS = 5 + 2 + 2 * 3 + 3 + 5 * 4

        @block.vector
        def _(dve):
            dve.sem_inc(bank_free, 3)
            dve.sem_inc(exps, 1)
            dve.sem_inc(o4_ready, 1)
            dve.sem_inc(m1_read, 1)
            dve.sem_inc(m1_filled, 1)
            dve.sem_inc(l_ready, 4)
            dve.sem_inc(turned, 4)
            dve.wait_ge(weights_in, 7 * 16)
            dve.wait_ge(const_ok, 14)
            with dve.Fori(0, B) as b:
                count, layers = [0], [0]

                def link(ins):
                    count[0] += 1
                    ins.then_inc(dve_seq, 1)
                    dve.wait_ge(dve_seq, b * LINKS + count[0])

                dve.wait_ge(hi_ready, b + 1)
                nc.vector.tensor_copy(V[:, 0:8, :, 0:D], SP_[:P, 0, :].rearrange("p (t h o) -> p t h o", h=H, o=D))
                nc.vector.tensor_copy(V[:, 8:12, :, 0:D], SP_[:P, 1, 0:4 * F].rearrange("p (t h o) -> p t h o", h=H, o=D)).then_inc(v_ready, 1)
                rest3 = REST[:, :].rearrange("p (a c) -> p a c", a=3)
                nc.vector.tensor_tensor(rest3, TP[:, :, 0:C], PARTS[:, 0, :].rearrange("p (a c) -> p a c", a=3),
                                        ALU.subtract).then_inc(rest_ready, 1)
                dve.wait_ge(mid_ready, b + 1)
                dve.wait_ge(rest_ready, b + 1)
                nc.vector.tensor_tensor(PARTS[:, 2, :], REST[:, :], PARTS[:, 1, :], ALU.subtract).then_inc(lo_ready, 1)

                with dve.Fori(0, NS) as s:
                    g = b * NS + s

                    def mask(j, c):
                        k = j % ST
                        if c == 0:
                            if j < ST:
                                dve.wait_ge(neg_ready, g * ST + k + 1)
                            dve.wait_ge(turned, g * TPS + j + 1)
                        dve.wait_ge(relus, g * (3 * TPS) + 3 * j + c + 1).then_inc(stood["dve"], 1)
                        nc.vector.tensor_tensor_reduce(out=L[:, j % 4, c * C:(c + 1) * C], in0=SP_[:P, c, 0:C],
                                                       in1=NEG[:, k, c * C:(c + 1) * C], scale=1.0, scalar=FLOOR,
                                                       op0=ALU.add, op1=ALU.max,
                                                       accum_out=CMAX[:, j % 4, c:c + 1]).then_inc(bank_free, 1)

                    def row_max(j):
                        dve.wait_ge(bank_free, g * (3 * TPS) + 3 * j + 3 + 3)
                        nc.vector.tensor_reduce(RMAX[:, j % 4:j % 4 + 1], CMAX[:, j % 4, :], AX.X, ALU.max).then_inc(rmax_ok, 1)

                    def shift(j):
                        dve.wait_ge(rmax_ok, g * TPS + j + 1)
                        m = RMAX[:, j % 4:j % 4 + 1]
                        nc.vector.scalar_tensor_tensor(out=SHIFT[:, j % 4:j % 4 + 1], in0=m, scalar=5.0, in1=m,
                                                       op0=ALU.mult, op1=ALU.max).then_inc(shift_ok, 1)

                    def leaky(j):
                        dve.wait_ge(shift_ok, g * TPS + j + 1)
                        nc.vector.scalar_tensor_tensor(out=L[:, j % 4, :], in0=L[:, j % 4, :],
                                                       scalar=SHIFT[:, j % 4:j % 4 + 1], in1=R[:, j % 4, :],
                                                       op0=ALU.subtract, op1=ALU.add).then_inc(l_ready, 1)

                    def keep_adj(n):
                        dve.wait_ge(m1_filled, g * 8 + n + 1 + 1)
                        k = {0: 0, 1: 1, 3: 2, 5: 3}[n]
                        words = AT[:, :, :, :].rearrange("p q n k -> p (q n k)").bitcast(f32).rearrange("p (q n) -> p q n", q=NS)
                        nc.vector.tensor_copy(words[:, :, bass.ds(s * C + k * P, P)],
                                              M1[:P, 0:NS * P].rearrange("p (q n) -> p q n", q=NS)).then_inc(m1_read, 1)

                    def keep_out(h, n):
                        dve.wait_ge(m1_filled, g * 8 + n + 1 + 1)
                        nc.vector.tensor_copy(OS[:, bass.ds(s * ST, ST), h, :],
                                              M1[:P, 0:ST * VW].rearrange("p (k o) -> p k o", k=ST)[:, :, 0:D + 1]).then_inc(m1_read, 1)

                    for c in range(3):
                        mask(0, c)
                    for j in range(TPS):
                        h, k = divmod(j, ST)
                        nxt = j + 1 < TPS
                        if nxt:
                            mask(j + 1, 0)
                        row_max(j)
                        if nxt:
                            mask(j + 1, 1)
                        shift(j)
                        if nxt:
                            mask(j + 1, 2)
                        leaky(j)
                        if k == 1:
                            keep_adj((0, 1, 3, 5)[h])
                        if k == 3 and h:
                            keep_out(h - 1, (2, 4, 6)[h - 1])
                    keep_out(H - 1, 7)

                def layer_norm():
                    mean = MEAN[:, :].unsqueeze(2).to_broadcast([P, NT, F])
                    rstd = RSTD[:, :].unsqueeze(2).to_broadcast([P, NT, F])
                    link(nc.vector.tensor_reduce(MEAN[:, :], Y[:, :, :], AX.X, ALU.add))
                    link(nc.vector.tensor_scalar(MEAN[:, :], MEAN[:, :], 1.0 / F, None, ALU.mult))
                    link(nc.vector.tensor_tensor(Y[:, :, :], Y[:, :, :], mean, ALU.subtract))
                    link(nc.vector.tensor_tensor(X[:, :, :], Y[:, :, :], Y[:, :, :], ALU.mult))
                    link(nc.vector.tensor_reduce(RSTD[:, :], X[:, :, :], AX.X, ALU.add))
                    nc.vector.tensor_scalar(RSTD[:, :], RSTD[:, :], 1.0 / F, EPS, ALU.mult, ALU.add).then_inc(var_ok, 1)
                    dve.wait_ge(rstd_ok, b * 4 + layers[0] + 1)
                    nc.vector.tensor_tensor(X[:, :, :], Y[:, :, :], rstd, ALU.mult).then_inc(x_ready, 1)
                    layers[0] += 1
                    dve.wait_ge(x_ready, b * 4 + layers[0])

                dve.wait_ge(m1_read, b * (8 * NS) + 8 * NS + 1)
                link(nc.vector.tensor_scalar(RSUM[:, :, :], OS[:, :, :, D], 1e-30, None, ALU.max))
                link(nc.vector.reciprocal(RSUM[:, :, :], RSUM[:, :, :]))
                link(nc.vector.tensor_tensor(Y[:, :, :].rearrange("p t (h o) -> p (t h) o", h=H),
                                             OS[:, :, :, 0:D].rearrange("p t h o -> p (t h) o"),
                                             RSUM[:, :, :].rearrange("p t h -> p (t h)").unsqueeze(2).to_broadcast([P, NT * H, D]),
                                             ALU.mult))
                link(nc.vector.tensor_tensor(Y[:, :, :], Y[:, :, :], B0[:, :].unsqueeze(1).to_broadcast([P, NT, F]), ALU.add))
                link(nc.vector.scalar_tensor_tensor(out=Y[:, :, :], in0=Y[:, :, :], scalar=0.0, in1=X[:, :, :],
                                                    op0=ALU.max, op1=ALU.add))
                layer_norm()
                dve.wait_ge(deg_psum, b + 1)
                link(nc.vector.tensor_scalar(RDEN[:, :], M1[:P, 0:NT], 1.0, None, ALU.add))
                link(nc.vector.reciprocal(RDEN[:, :], RDEN[:, :]))
                for l in range(3):
                    dve.wait_ge(xh_ready, b * 3 + l + 1)
                    nc.vector.tensor_tensor(XP[:, :, F:2 * F], X[:, :, :], XP[:, :, 0:F], ALU.subtract).then_inc(parts_ready, 1)
                    dve.wait_ge(y_psum, b * 3 + l + 1)
                    for t0, t1 in ((0, 8), (8, NT)):
                        nt = t1 - t0
                        ps = TP[:P, t0 // 8, 0:nt * F].rearrange("p (t f) -> p t f", f=F)
                        y, xx = Y[:, t0:t1, :], X[:, t0:t1, :]
                        if l == 0:
                            nc.vector.tensor_tensor(y, ps, xx, ALU.add).then_inc(dve_seq, 1)
                        elif l == 1:
                            nc.vector.tensor_tensor(y, ps, xx, ALU.add).then_inc(dve_seq, 1)
                        else:
                            nc.vector.scalar_tensor_tensor(out=y, in0=ps, scalar=0.5, in1=xx, op0=ALU.is_gt,
                                                           op1=ALU.add).then_inc(dve_seq, 1)
                        count[0] += 1
                    dve.wait_ge(dve_seq, b * LINKS + count[0])
                    if l == 0:
                        link(nc.vector.tensor_tensor(Y[:, :, :], Y[:, :, :], RDEN[:, :].unsqueeze(2).to_broadcast([P, NT, F]), ALU.mult))
                        link(nc.vector.tensor_tensor(Y[:, :, :], Y[:, :, :], X[:, :, :], ALU.add))
                    elif l == 1:
                        link(nc.vector.tensor_tensor(Y[:, :, :], Y[:, :, :], B2[:, :].unsqueeze(1).to_broadcast([P, NT, F]), ALU.add))
                    layer_norm()
                assert count[0] == LINKS, count[0]


_INS = ['x', 'adj', 'L0_gnn_kernel', 'L0_gnn_attention_kernel', 'L0_gnn_attention_kernel_2', 'L0_gnn_bias',
        'L2_gnn_weight', 'L2_gnn_bias']


def kernel(**inputs):
    import numpy as _np
    import concourse.bacc as _bacc
    from concourse import mybir as _mybir
    from concourse.bass_utils import run_bass_kernel_spmd as _run

    nc = _bacc.Bacc("TRN2", target_bir_lowering=False, num_devices=1)
    arrays, args = {}, []
    for name in _INS:
        a = _np.ascontiguousarray(inputs[name])
        arrays[f"in_{name}_dram"] = a
        args.append(nc.dram_tensor(f"in_{name}_dram", a.shape, _mybir.dt.from_np(a.dtype), kind="ExternalInput").ap())
    out = nc.dram_tensor("out_0_dram", (B, N, F), _mybir.dt.float32, kind="ExternalOutput").ap()
    adj_resnorm(nc, *args, out)
    r = _run(nc, [arrays], core_ids=[0])
    return r.results[0]["out_0_dram"]
```

```python
import concourse.bass as bass
from concourse import mybir
from contextlib import ExitStack

B, N, F = 8, 1500, 64
H, D = 4, 16
P = 125
NT = N // P
ST = 4
NS = NT // ST
C = ST * P
NG = B * NS
TPS = H * ST
TPG = NS * TPS
UPG = NS * H
RS, LS, NGS = 3, 3, 6
VW = 32
TERMS = [(0, 0), (0, 1), (0, 2), (1, 0), (1, 1), (2, 0)]
KS = len(TERMS) * D
BIG = 2.0 ** 30
FLOOR = -1.0e6
EPS = 1e-5


CONSTS = 14
LINKS = 5 + 4 * 4 + 3 * 2 + 3
PLACES = {(5, 2): "sums", (6, 0): "reciprocal", (6, 1): "divide", (6, 2): "bias", (7, 0): "residual",
          (10, 2): ("scale", 0), (12, 2): ("x_low", 0), (21, 2): ("scale", 1), (23, 2): ("x_low", 1),
          (33, 2): ("scale", 2), (35, 2): ("x_low", 2), (47, 2): ("scale", 3)}
for at in (7, 18, 29, 43):
    PLACES.update({(at, 2): "mean", (at + 1, 0): "centre", (at + 1, 1): "square", (at + 2, 0): "add_squares",
                   (at + 2, 1): "variance"})
X_HIGH = [11, 22, 34]
DEGREES_AT = 37
POWERS = [(0, 1), (0, 3), (1, 3), (2, 2)]
AT0, ATN = 43, 5
NARROW_AT = [8, 26, 44]


def masked_by_pe(j):
    return j in {1, 2, 3, 4, 5, 6, 7, 8, 9, 10, 19, 20, 21, 22, 23, 24, 30, 31, 32, 33, 34, 35, 37, 44, 45, 46, 47}


def adj_resnorm(nc, x, adj, wv, wself, wother, bias0, w2, bias2, out):
    f32, bf16, f16, f8 = mybir.dt.float32, mybir.dt.bfloat16, mybir.dt.float16, mybir.dt.float8e4
    ALU, ACT, AX = mybir.AluOpType, mybir.ActivationFunctionType, mybir.AxisListType

    x_v = x.rearrange("b (s i k) f -> b i s k f", i=P, k=ST)
    out_v = out.rearrange("b (s i k) f -> b i s k f", i=P, k=ST)
    adj_v = adj.rearrange("b (s i k) m -> b s k i m", i=P, k=ST)

    ctx = ExitStack()
    with ctx:
        def sb(name, shape, dt):
            return ctx.enter_context(nc.sbuf_tensor(name, shape, dt))

        def sem(name):
            return ctx.enter_context(nc.semaphore(name))

        A = sb("A", [P, ST, N], bf16)
        A8 = sb("A8", [P, NT, N], f8)
        NEG = sb("NEG", [P, NGS, N], bf16)
        AT = sb("AT", [P, NS, N, ST], f8)
        FS = sb("FS", [KS, H, C], bf16)
        FO = sb("FO", [KS, H, N], bf16)
        R = sb("R", [P, RS, N], f32)
        L = sb("L", [P, LS, N], f32)
        PT = sb("PT", [P, 2, NT, C], f32)
        V = sb("V", [P, NT, H, D + 1], f32)
        VN = sb("VN", [P, NT, H, D], f32)
        XT = sb("XT", [F, C], f32)
        PARTS = sb("PARTS", [128, 3, N], bf16)
        REST = sb("REST", [128, C], f32)
        YT = sb("YT", [128, C], f32)
        O4 = sb("O4", [128, C], f32)
        OS = sb("OS", [P, NT, H, D + 1], f32)
        XIN = sb("XIN", [P, NT, F], f32)
        X = sb("X", [P, NT, F], f32)
        Y = sb("Y", [P, NT, F], f32)
        XP = sb("XP", [P, NT, 2 * F], f16)
        SQ = XP[:, :, :].rearrange("p t f -> p (t f)").bitcast(f32).rearrange("p (t f) -> p t f", f=F)
        DEG = sb("DEG", [P, NT], f32)
        RDEN = sb("RDEN", [P, NT], f32)
        RSUM = sb("RSUM", [P, NT, H], f32)
        MEAN = sb("MEAN", [P, NT], f32)
        RSTD = sb("RSTD", [P, NT], f32)
        CMAX = sb("CMAX", [P, 4, 3], f32)
        RMAX = sb("RMAX", [P, 4], f32)
        SHIFT = sb("SHIFT", [P, 4], f32)
        WV = sb("WV", [F, H, D], f32)
        WA = sb("WA", [F, 2, H, D], f32)
        WW = sb("WW", [128, 2, F], f32)
        B0 = sb("B0", [P, F], f32)
        B2 = sb("B2", [P, F], f32)
        ID = sb("ID", [128, 128], f32)
        IDB = sb("IDB", [128, 128], bf16)
        E4 = sb("E4", [128, D + 1], f32)
        NHALF = sb("NHALF", [P, NT], f32)

        SP_ = ctx.enter_context(nc.psum_tensor("SP_", [128, 3, 512], f32))
        TP = ctx.enter_context(nc.psum_tensor("TP", [128, 3, 512], f32))
        M0 = ctx.enter_context(nc.psum_tensor("M0", [128, 512], f32))
        M1 = ctx.enter_context(nc.psum_tensor("M1", [128, 512], f32))

        weights_in = sem("weights_in")
        const_ok = sem("const_ok")
        x_in = sem("x_in")
        a_in = [sem(f"a_in{k}") for k in range(ST)]
        fs_in = [sem(f"fs_in{h}") for h in range(H)]
        fo_in = [sem(f"fo_in{h}") for h in range(H)]
        a8_ready = sem("a8_ready")
        neg_ready = sem("neg_ready")
        scores = sem("scores")
        relus = sem("relus")
        bank_free = sem("bank_free")
        rmax_ok = sem("rmax_ok")
        shift_ok = sem("shift_ok")
        l_ready = sem("l_ready")
        turned = sem("turned")
        exps = sem("exps")
        v_ready = sem("v_ready")
        pv_done = sem("pv_done")
        o4_ready = sem("o4_ready")
        ot_done = sem("ot_done")
        os_kept = sem("os_kept")
        m1_filled = sem("m1_filled")
        m1_read = sem("m1_read")
        hi_ready = sem("hi_ready")
        mid_ready = sem("mid_ready")
        lo_ready = sem("lo_ready")
        dve_seq = sem("dve_seq")
        deg_ok = sem("deg_ok")
        rden_ok = sem("rden_ok")
        var_ok = sem("var_ok")
        rstd_ok = sem("rstd_ok")
        x_ready = sem("x_ready")
        xh_ready = sem("xh_ready")
        xp_ready = sem("xp_ready")
        stored = sem("stored")
        stood = {e: sem(f"stood_{e}") for e in ("pe", "act", "dve", "pool")}
        block = ctx.enter_context(nc.Block())

        def three(ap):
            return ap.rearrange("p (a c) -> p a c", a=3)

        LAYER_AT = [(12, 0), (23, 1), (37, 2)]
        LATE = [(t - ATN, ("AT", t)) for t in range(ATN, NT)]
        LAYERS = [(at + 2 * c + d, (kind, l, c)) for at, l in LAYER_AT for c in range(3) for d, kind in enumerate("YW")]
        NEXT = [(18, ("XT", 0)), (19, ("FE", 0)), (20, ("FT", 0)), (29, ("XT", 1)), (30, ("FE", 1)), (31, ("FT", 1)),
                (33, ("XT", 2)), (34, ("FE", 2)), (35, ("FT", 2))]
        EARLY = [(AT0 + t, ("AT", t)) for t in range(ATN)]
        FULL = sorted(LATE + LAYERS + NEXT + EARLY)
        FIRST = sorted(NEXT + EARLY)
        LAST = sorted(LATE + LAYERS)
        PRE = [("XT", 0), ("FE", 0), ("FT", 0), ("XT", 1), ("FE", 1), ("FT", 1), ("XT", 2), ("FE", 2), ("FT", 2)]
        assert len({at for at, _ in FULL}) == len(FULL) and FULL[-1][0] == TPG - 1

        def task_number(b, tasks, task):
            n = [x for _, x in tasks].index(task)
            if tasks is FIRST:
                return len(PRE) + n
            return (b - 1) * len(FULL) + (len(PRE) + len(FIRST) + n)

        def tasks_of(b, kind):
            return {"first": FIRST, "full": FULL, "last": LAST}[kind]

        def unit_of(b, kind, u):
            if u >= 0:
                return (b, u) if kind != "last" else None
            return (b - 1, UPG + u) if kind != "first" else None

        NF = len(TERMS)

        @block.sync
        def _(sp):
            def load_parts(dst, sem_, side, h, cols):
                for n, pair in enumerate(TERMS):
                    sp.dma_start(dst[n * D:(n + 1) * D],
                                 PARTS[side * F + h * D:side * F + (h + 1) * D, pair[side], cols]).then_inc(sem_, 16)

            def load_x(dst, b, sem_):
                sp.dma_start(dst[:, :, :].rearrange("p (s k) f -> p s k f", k=ST), x_v[b]).then_inc(sem_, 16)

            def store(b):
                sp.wait_ge(x_ready, b * 4 + 4)
                sp.dma_start(out_v[b], X[:, :, :].rearrange("p (s k) f -> p s k f", k=ST)).then_inc(stored, 16)

            def graph(b, layers):
                for s in range(NS):
                    for h in range(H):
                        sp.wait_ge(scores, b * (3 * TPG) + 3 * (s * TPS + ST * h + ST))
                        if s == NS - 1:
                            if h == 0:
                                sp.wait_ge(lo_ready, b * 3 + 6)
                            load_parts(FO[:, h, :], fo_in[h], 1, h, slice(0, N))
                        sn = (s + 1) % NS
                        load_parts(FS[:, h, :], fs_in[h], 0, h, slice(sn * C, (sn + 1) * C))
                        if s == NS - 1 and h == 0:
                            load_x(XIN, b, x_in)
                        if layers and s == 0 and h == 0:
                            sp.wait_ge(dve_seq, (b - 1) * LINKS + 5)
                            load_x(XIN, (b + 1) % B, x_in)
                if layers:
                    store(b - 1)

            sp.sem_inc(stored, 16)
            load_x(XIN, 0, x_in)
            sp.dma_start(WV[:, :, :], wv.rearrange("h f o -> f h o")).then_inc(weights_in, 16)
            sp.dma_start(WA[:, 0, :, :], wself.rearrange("h f o -> f h o")).then_inc(weights_in, 16)
            sp.dma_start(WA[:, 1, :, :], wother.rearrange("h f o -> f h o")).then_inc(weights_in, 16)
            sp.dma_start(WW[0:F, 1, :], w2).then_inc(weights_in, 16)
            sp.dma_start(WW[F:2 * F, 1, :], w2).then_inc(weights_in, 16)
            sp.dma_start(B0[:, :], bias0.rearrange("a b h o -> (a b h o)").partition_broadcast(P)).then_inc(weights_in, 16)
            sp.dma_start(B2[:, :], bias2.partition_broadcast(P)).then_inc(weights_in, 16)
            sp.wait_ge(lo_ready, 3)
            for h in range(H):
                load_parts(FO[:, h, :], fo_in[h], 1, h, slice(0, N))
                load_parts(FS[:, h, :], fs_in[h], 0, h, slice(0, C))
            load_x(XIN, 1, x_in)
            graph(0, False)
            with sp.Fori(1, B) as b:
                graph(b, True)
            store(B - 1)
            for h in range(H):
                sp.wait_ge(fs_in[h], 16 * NF * (NG + 1))
                sp.wait_ge(fo_in[h], 16 * NF * (B + 1))
            sp.wait_ge(x_in, 16 * (2 * B + 1))
            sp.wait_ge(stored, 16 * B + 16)

        @block.gpsimd
        def _(pool):
            made = [0]

            def const(ins):
                ins.then_inc(const_ok, 1)
                made[0] += 1
                pool.wait_ge(const_ok, made[0])

            for t in (ID, IDB, E4):
                const(nc.gpsimd.memset(t[:, :], 0.0))
            const(nc.gpsimd.memset(WW[:, 0, :], 0.0))
            const(nc.gpsimd.memset(NHALF[:, :], -0.5))
            const(nc.gpsimd.memset(V[:, :, :, D:D + 1], 1.0))

            def ones(ap, base, cols):
                const(nc.gpsimd.affine_select(out=ap, in_=ap, compare_op=ALU.not_equal, fill=1.0, base=-base,
                                              pattern=[[-1, cols]], channel_multiplier=1))

            ones(ID[:, :], 0, 128)
            ones(IDB[:, :], 0, 128)
            for c in range(4):
                ones(E4[:, :], VW * c, D + 1)
            for c in range(2):
                ones(WW[:, 0, :], F * c, F)
            assert made[0] == CONSTS

            def load(b, s, k):
                pool.dma_start(A[:, k, :], adj_v[b, s, k]).then_inc(a_in[k], 16)

            def negate(t, k):
                nc.gpsimd.tensor_scalar(NEG[:, t % NGS, :].rearrange("p (s k i) -> p s i k", k=ST, i=P),
                                        A[:, k, :].rearrange("p (s i k) -> p s i k", i=P, k=ST),
                                        -1.0, BIG, ALU.add, ALU.mult).then_inc(neg_ready, 1)

            def power(n):
                pool.wait_ge(var_ok, n + 1)
                nc.gpsimd.tensor_tensor(RSTD[:, :], RSTD[:, :], NHALF[:, :], ALU.pow).then_inc(rstd_ok, 1)

            def graph(b, layers):
                for s in range(NS):
                    g = b * NS + s
                    t0 = (s + 1) % NS * ST
                    for k in range(ST):
                        pool.wait_ge(a8_ready, g * ST + k + 1)
                        pool.wait_ge(neg_ready, g * ST + k + 1)
                        load(b if s + 1 < NS else (b + 1) % B, (s + 1) % NS, k)
                    for k in range(ST):
                        if k >= 2:
                            pool.wait_ge(bank_free, b * (3 * TPG) + 3 * (s * TPS + TPS - ST + k - 2) + 3 + 3)
                        elif layers or s > 0:
                            pool.wait_ge(bank_free, b * (3 * TPG) + 3 * (s * TPS - ST + k + 2) + 3 + 3)
                        pool.wait_ge(a_in[k], g * 16 + 32).then_inc(stood["pool"], 1)
                        negate(t0 + k, k)
                        for n, place in enumerate(POWERS):
                            if layers and place == (s, k):
                                power((b - 1) * 4 + n)

            for k in range(ST):
                load(0, 0, k)
            for k in range(ST):
                pool.wait_ge(a_in[k], 16)
                negate(k, k)
            graph(0, False)
            with pool.Fori(1, B) as b:
                graph(b, True)
            for n in range(4):
                power((B - 1) * 4 + n)
            for k in range(ST):
                pool.wait_ge(a_in[k], 16 * (NG + 1))

        @block.tensor
        def _(pe):
            pe.wait_ge(weights_in, 7 * 16)
            pe.wait_ge(const_ok, CONSTS)

            def score(b, j, c):
                s, i = divmod(j % TPG, TPS)
                h, k = divmod(i, ST)
                g = b * NS + j // TPS
                if k == 0 and c == 0:
                    pe.wait_ge(fs_in[h], g * (16 * NF) + 16 * NF)
                    if s == 0:
                        pe.wait_ge(fo_in[h], b * (16 * NF) + 16 * NF * (j // TPG + 1))
                pe_mask = masked_by_pe(j % TPG)
                if c == 0 and pe_mask:
                    pe.wait_ge(neg_ready, g * ST + k + 1)
                pe.wait_ge(bank_free, b * (3 * TPG) + 3 * j + c + 1)
                ins = nc.tensor.matmul(SP_[:P, c, 0:C], FS[:, h, k * P:(k + 1) * P], FO[:, h, c * C:(c + 1) * C],
                                       start=True, stop=not pe_mask)
                if pe_mask:
                    ins = nc.tensor.matmul(SP_[:P, c, 0:C], IDB[:P, :P],
                                           NEG[:, (s * ST + k) % NGS, c * C:(c + 1) * C], start=False, stop=True)
                ins.then_inc(scores, 1)

            def turn(b, j, half):
                if half == 0:
                    pe.wait_ge(l_ready, b * TPG + j + 1 + RS)
                    pe.wait_ge(exps, b * TPG + j + 1)
                for m in range(half * NT // 2, (half + 1) * NT // 2):
                    last = nc.tensor.transpose(TP[:P, m // 4, m % 4 * P:(m % 4 + 1) * P],
                                               L[:, j % LS, m * P:(m + 1) * P], ID[:P, :P])
                if half == 1:
                    last.then_inc(turned, 1)

            def weigh(b, u, r):
                h = u % H
                if r == 0:
                    pe.wait_ge(exps, b * TPG + ST * u + ST + 1)
                    pe.wait_ge(os_kept, b * UPG + u + 1)
                    if u == 0:
                        pe.wait_ge(v_ready, b + 1)
                for c in range(4):
                    last = nc.tensor.matmul(M0[VW * c:VW * c + D + 1, 0:C], V[:, 3 * c + r, h, :],
                                            PT[:, h % 2, 3 * c + r, :], start=(r == 0), stop=(r == 2))
                if r == 2:
                    last.then_inc(pv_done, 1)

            def gather(b, u):
                pe.wait_ge(o4_ready, b * UPG + u + 1)
                for k in range(ST):
                    last = nc.tensor.matmul(M0[:P, k * VW:k * VW + D + 1], O4[:, k * P:(k + 1) * P], E4[:, :],
                                            start=True, stop=True)
                last.then_inc(ot_done, 1)

            def collect(c, m0, m1):
                for m in range(m0, m1):
                    last = nc.tensor.matmul(M1[:, 0:C], XP[:, m, :], AT[:, m // ST, c * C:(c + 1) * C, m % ST],
                                            start=(m == 0), stop=(m == NT - 1))
                return last

            def m1_task(b, n, task):
                if task[0] == "AT":
                    t = task[1]
                    pe.wait_ge(rden_ok, (b if t < ATN else b - 1) + 1)
                elif task[0] == "Y":
                    pe.wait_ge(xp_ready, (b - 1) * 3 + task[1] + 1)
                    pe.wait_ge(m1_read, n + 1).then_inc(stood["pe"], 1)
                    collect(task[-1], 0, 6)
                    return
                elif task[0] == "XT":
                    pe.wait_ge(x_in, b * 32 + 32)
                pe.wait_ge(m1_read, n + 1).then_inc(stood["pe"], 1)
                fill_m1(task).then_inc(m1_filled, 1)

            def fill_m1(task):
                kind, c = task[0], task[-1]
                if kind == "AT":
                    words = A8[:, c, :].bitcast(f32)
                    for q in range(NS):
                        last = nc.tensor.transpose(M1[:P, q * P:(q + 1) * P], words[:, q * P:(q + 1) * P], ID[:P, :P])
                elif kind == "W":
                    for k in range(ST):
                        last = nc.tensor.matmul(M1[:P, k * F:(k + 1) * F], YT[:, k * P:(k + 1) * P],
                                                WW[:, 1 if task[1] == 1 else 0, :], start=True, stop=True)
                elif kind == "XT":
                    for k in range(ST):
                        last = nc.tensor.transpose(M1[:F, k * P:(k + 1) * P], XIN[:, ST * c + k, :], ID[:P, :P])
                elif kind == "FE":
                    for k in range(ST):
                        last = nc.tensor.matmul(M1[:P, k * F:(k + 1) * F], XT[:, k * P:(k + 1) * P],
                                                WV[:, :, :].rearrange("f h o -> f (h o)"), start=True, stop=True)
                else:
                    last = nc.tensor.matmul(M1[:, 0:C], WA[:, :, :, :].rearrange("f s h o -> f (s h o)"), XT[:, :],
                                            start=True, stop=True)
                return last

            pe.wait_ge(x_in, 16)
            for n, task in enumerate(PRE):
                pe.wait_ge(m1_read, n + 1)
                fill_m1(task).then_inc(m1_filled, 1)
            for j in range(2):
                for c in range(3):
                    score(0, j, c)

            def graph(b, kind):
                tasks = tasks_of(b, kind)
                at = dict(tasks)
                for j in range(TPG):
                    back = (b, j - 1) if j else (b - 1, TPG - 1)
                    turns = (kind != "first" or j) and (kind != "last" or j == 0)
                    for c in range(3):
                        if kind != "last":
                            score(b, j + 2, c)
                        before = at.get(j - 1)
                        if c < 2 and before and before[0] == "Y":
                            last = collect(before[-1], 6 + 3 * c, 9 + 3 * c)
                            if c == 1:
                                last.then_inc(m1_filled, 1)
                        if turns and c < 2:
                            turn(*back, c)
                    if j % ST:
                        unit = unit_of(b, kind, (j - 1) // ST - 1)
                        if unit:
                            weigh(*unit, j % ST - 1)
                    else:
                        unit = unit_of(b, kind, j // ST - 2)
                        if unit:
                            gather(*unit)
                    if j in at:
                        m1_task(b, task_number(b, tasks, at[j]), at[j])

            graph(0, "first")
            with pe.Fori(1, B) as b:
                graph(b, "full")
            graph(B, "last")

        @block.scalar
        def _(act):
            def relu(b, j, c):
                if c == 0:
                    act.wait_ge(l_ready, b * TPG + j + 1)
                act.wait_ge(scores, b * (3 * TPG) + 3 * j + c + 1)
                nc.scalar.activation(R[:, j % RS, c * C:(c + 1) * C], SP_[:P, c, 0:C], ACT.Relu,
                                     scale=4.0).then_inc(relus, 1)

            def expo(b, j):
                h, k = j // ST % H, j % ST
                act.wait_ge(turned, b * TPG + j + 1 + LS)
                nc.scalar.activation(PT[:, h % 2, :, k * P:(k + 1) * P].rearrange("p (a m) n -> p a m n", a=3),
                                     TP[:P, :, 0:C].rearrange("p a (m n) -> p a m n", m=4), ACT.Exp,
                                     scale=0.05).then_inc(exps, 1)

            def take(b, u):
                act.wait_ge(pv_done, b * UPG + u + 1)
                nc.scalar.activation(O4[:, :], M0[:, 0:C], ACT.Copy).then_inc(o4_ready, 1)

            def narrow(b, g, t):
                act.wait_ge(a_in[t % ST], g * 16 + 16).then_inc(stood["act"], 1)
                nc.scalar.activation(A8[:, t, :], A[:, t % ST, :], ACT.Copy, accum_out=DEG[:, t:t + 1],
                                     saturate=False).then_inc(a8_ready, 1)

            def values(b):
                nc.scalar.activation(V[:, :, :, 0:D], VN[:, :, :, :], ACT.Copy).then_inc(v_ready, 1)

            def read_m1(n, task):
                kind, c = task[0], task[-1]
                act.wait_ge(m1_filled, n + 1)
                if kind == "XT":
                    ins = nc.scalar.activation(XT[:, :], M1[:F, 0:C], ACT.Copy)
                elif kind == "FE":
                    ins = nc.scalar.activation(VN[:, ST * c:ST * (c + 1), :, :],
                                               M1[:P, 0:ST * F].rearrange("p (t h o) -> p t h o", h=H, o=D), ACT.Copy)
                else:
                    ins = nc.scalar.activation(YT[:, :], M1[:, 0:C], ACT.Copy)
                ins.then_inc(m1_read, 1)

            def high(n, c):
                act.wait_ge(m1_filled, n + 1)
                nc.scalar.activation(PARTS[:, 0, c * C:(c + 1) * C], M1[:, 0:C], ACT.Copy).then_inc(hi_ready, 1)

            def middle(n, c):
                act.wait_ge(m1_read, n + 2)
                nc.scalar.activation(PARTS[:, 1, c * C:(c + 1) * C], REST[:, :], ACT.Copy).then_inc(mid_ready, 1)

            def graph(b, kind):
                tasks = tasks_of(b, kind)
                at = dict(tasks)
                for j in range(TPG):
                    if kind != "last":
                        relu(b, j + 2, 0)
                        relu(b, j + 2, 1)
                    unit = unit_of(b, kind, j // ST - 2) if j % ST == 0 else None
                    if unit:
                        take(*unit)
                    task = at.get(j - 1)
                    if task and task[0] in ("XT", "FE", "Y"):
                        read_m1(task_number(b, tasks, task), task)
                    if task and task[0] == "FT":
                        if task[1] == NS - 1:
                            for h in (2, 3):
                                act.wait_ge(fs_in[h], b * (NS * 16 * NF) + NS * 16 * NF)
                        high(task_number(b, tasks, task), task[1])
                    task = at.get(j - 3)
                    if task and task[0] == "FT":
                        middle(task_number(b, tasks, task), task[1])
                    if j in X_HIGH and kind != "first":
                        act.wait_ge(x_ready, (b - 1) * 4 + X_HIGH.index(j) + 1)
                        nc.scalar.activation(XP[:, :, 0:F], X[:, :, :], ACT.Copy).then_inc(xh_ready, 1)
                    if kind != "last":
                        if j == ST:
                            act.wait_ge(m1_read, (len(PRE) if kind == "first" else task_number(b, tasks, LATE[0][1])) + 1)
                            values(b)
                    if (kind != "first" or j) and (kind != "last" or j == 0):
                        expo(b, j - 1) if j else expo(b - 1, TPG - 1)
                    if kind != "last":
                        relu(b, j + 2, 2)
                        if 0 <= j - NARROW_AT[j // TPS] < ST:
                            t = (j // TPS + 1) % NS * ST + j - NARROW_AT[j // TPS]
                            if j // TPS == NS - 1:
                                act.wait_ge(rden_ok, b + 1)
                                act.wait_ge(m1_filled, task_number(b, tasks, ("AT", t)) + 1)
                            narrow(b, b * NS + j // TPS + 1, t)

            for c in range(3):
                for d, kind in enumerate(("XT", "FE")):
                    read_m1(3 * c + d, (kind, c))
                high(3 * c + 2, c)
                middle(3 * c + 2, c)
            for t in range(ST):
                narrow(0, 0, t)
            for j in range(2):
                for c in range(3):
                    relu(0, j, c)
            graph(0, "first")
            with act.Fori(1, B) as b:
                graph(b, "full")
            graph(B, "last")

        @block.vector
        def _(dve):
            dve.sem_inc(bank_free, 3)
            dve.sem_inc(l_ready, RS)
            dve.sem_inc(turned, LS)
            dve.sem_inc(exps, 1)
            dve.sem_inc(m1_read, 1)
            nc.vector.memset(M0[:, :], 0.0).then_inc(os_kept, 1)
            dve.wait_ge(weights_in, 7 * 16)
            dve.wait_ge(const_ok, CONSTS)

            def mask(b, j, c):
                s, i = divmod(j % TPG, TPS)
                h, k = divmod(i, ST)
                if c == 0:
                    dve.wait_ge(turned, b * TPG + j + 1)
                    if h == 0:
                        dve.wait_ge(neg_ready, (b * NS + j // TPS) * ST + k + 1)
                dve.wait_ge(relus, b * (3 * TPG) + 3 * j + c + 1).then_inc(stood["dve"], 1)
                if masked_by_pe(j % TPG):
                    in1 = R[:, j % RS, c * C:(c + 1) * C]
                else:
                    in1 = NEG[:, (s * ST + k) % NGS, c * C:(c + 1) * C]
                nc.vector.tensor_tensor_reduce(out=L[:, j % LS, c * C:(c + 1) * C], in0=SP_[:P, c, 0:C],
                                               in1=in1, scale=1.0, scalar=FLOOR, op0=ALU.add, op1=ALU.max,
                                               accum_out=CMAX[:, j % 4, c:c + 1]).then_inc(bank_free, 1)

            def row_max(b, j):
                dve.wait_ge(bank_free, b * (3 * TPG) + 3 * j + 3 + 3)
                nc.vector.tensor_reduce(RMAX[:, j % 4:j % 4 + 1], CMAX[:, j % 4, :], AX.X, ALU.max).then_inc(rmax_ok, 1)

            def shift(b, j):
                dve.wait_ge(rmax_ok, b * TPG + j + 1)
                m = RMAX[:, j % 4:j % 4 + 1]
                if masked_by_pe(j % TPG):
                    nc.vector.tensor_copy(SHIFT[:, j % 4:j % 4 + 1], m).then_inc(shift_ok, 1)
                else:
                    nc.vector.scalar_tensor_tensor(out=SHIFT[:, j % 4:j % 4 + 1], in0=m, scalar=5.0, in1=m,
                                                   op0=ALU.mult, op1=ALU.max).then_inc(shift_ok, 1)

            def leaky(b, j):
                dve.wait_ge(shift_ok, b * TPG + j + 1)
                row, m = L[:, j % LS, :], SHIFT[:, j % 4:j % 4 + 1]
                if masked_by_pe(j % TPG):
                    nc.vector.tensor_scalar(row, row, m, None, ALU.subtract).then_inc(l_ready, 1)
                else:
                    nc.vector.scalar_tensor_tensor(out=row, in0=row, scalar=m, in1=R[:, j % RS, :],
                                                   op0=ALU.subtract, op1=ALU.add).then_inc(l_ready, 1)

            def keep(b, u):
                s, h = divmod(u, H)
                dve.wait_ge(ot_done, b * UPG + u + 1)
                nc.vector.tensor_copy(OS[:, s * ST:(s + 1) * ST, h, :],
                                      M0[:P, 0:ST * VW].rearrange("p (k o) -> p k o", k=ST)[:, :, 0:D + 1]).then_inc(os_kept, 1)

            def keep_adj(n, t):
                dve.wait_ge(m1_filled, n + 1)
                words = AT[:, :, :, :].rearrange("p q n k -> p (q n k)").bitcast(f32).rearrange("p (q n) -> p q n", q=NS)
                nc.vector.tensor_copy(words[:, :, t * P:(t + 1) * P],
                                      M1[:P, 0:NS * P].rearrange("p (q n) -> p q n", q=NS)).then_inc(m1_read, 1)

            def rest(hi, c):
                if not isinstance(hi, int) or hi > 1:
                    dve.wait_ge(lo_ready, hi - 1)
                dve.wait_ge(hi_ready, hi)
                nc.vector.tensor_tensor(REST[:, :], M1[:, 0:C], PARTS[:, 0, c * C:(c + 1) * C],
                                        ALU.subtract).then_inc(m1_read, 1)

            def low(mid, c):
                dve.wait_ge(mid_ready, mid)
                nc.vector.tensor_tensor(PARTS[:, 2, c * C:(c + 1) * C], REST[:, :], PARTS[:, 1, c * C:(c + 1) * C],
                                        ALU.subtract).then_inc(lo_ready, 1)

            bc3 = [P, NT, F]
            y3, x3 = Y[:, :, :], X[:, :, :]

            def degrees(b):
                dve.wait_ge(a8_ready, b * NT + NT)
                nc.vector.tensor_scalar(DEG[:, :], DEG[:, :], 1.0, None, ALU.add).then_inc(deg_ok, 1)
                dve.wait_ge(deg_ok, b + 1)
                nc.vector.reciprocal(RDEN[:, :], DEG[:, :]).then_inc(rden_ok, 1)

            class Layers:

                def __init__(self, b):
                    self.base, self.b, self.n = (b - 1) * LINKS, b - 1, 0

                def at(self, j, place):
                    step = PLACES.get((j, place))
                    if step:
                        name, *l = step if isinstance(step, tuple) else (step,)
                        {"sums": self.sums, "reciprocal": self.reciprocal, "divide": self.divide, "bias": self.bias,
                         "residual": self.residual, "mean": self.mean, "centre": self.centre, "square": self.square,
                         "add_squares": self.add_squares, "variance": self.variance, "scale": self.scale,
                         "x_low": self.x_low}[name](*l)

                def link(self, make):
                    if self.n:
                        dve.wait_ge(dve_seq, self.base + self.n).then_inc(stood["dve"], 1)
                    make().then_inc(dve_seq, 1)
                    self.n += 1

                def sums(self):
                    dve.wait_ge(os_kept, self.b * UPG + UPG + 1)
                    self.link(lambda: nc.vector.tensor_scalar(RSUM[:, :, :], OS[:, :, :, D], 1e-30, None, ALU.max))

                def reciprocal(self):
                    self.link(lambda: nc.vector.reciprocal(RSUM[:, :, :], RSUM[:, :, :]))

                def divide(self):
                    self.link(lambda: nc.vector.tensor_tensor(
                        y3.rearrange("p t (h o) -> p (t h) o", h=H), OS[:, :, :, 0:D].rearrange("p t h o -> p (t h) o"),
                        RSUM[:, :, :].rearrange("p t h -> p (t h)").unsqueeze(2).to_broadcast([P, NT * H, D]), ALU.mult))

                def bias(self):
                    self.link(lambda: nc.vector.tensor_tensor(y3, y3, B0[:, :].unsqueeze(1).to_broadcast(bc3), ALU.add))

                def residual(self):
                    dve.wait_ge(x_in, self.b * 32 + 48)
                    self.link(lambda: nc.vector.scalar_tensor_tensor(out=y3, in0=y3, scalar=0.0, in1=XIN[:, :, :],
                                                                     op0=ALU.max, op1=ALU.add))

                def mean(self):
                    self.link(lambda: nc.vector.tensor_reduce(MEAN[:, :], y3, AX.X, ALU.add))

                def centre(self):
                    self.link(lambda: nc.vector.scalar_tensor_tensor(
                        out=y3, in0=MEAN[:, :].unsqueeze(2).to_broadcast(bc3), scalar=-1.0 / F, in1=y3,
                        op0=ALU.mult, op1=ALU.add))

                def square(self):
                    self.link(lambda: nc.vector.tensor_tensor(SQ, y3, y3, ALU.mult))

                def add_squares(self):
                    self.link(lambda: nc.vector.tensor_reduce(RSTD[:, :], SQ, AX.X, ALU.add))

                def variance(self):
                    dve.wait_ge(dve_seq, self.base + self.n).then_inc(stood["dve"], 1)
                    nc.vector.tensor_scalar(RSTD[:, :], RSTD[:, :], 1.0 / F, EPS, ALU.mult, ALU.add).then_inc(var_ok, 1)

                def scale(self, l):
                    dve.wait_ge(rstd_ok, self.b * 4 + l + 1)
                    if l == 0:
                        dve.wait_ge(stored, self.b * 16 + 16)
                    nc.vector.tensor_tensor(x3, y3, RSTD[:, :].unsqueeze(2).to_broadcast(bc3), ALU.mult).then_inc(x_ready, 1)

                def x_low(self, l):
                    dve.wait_ge(xh_ready, self.b * 3 + l + 1)
                    nc.vector.tensor_tensor(XP[:, :, F:2 * F], x3, XP[:, :, 0:F], ALU.subtract).then_inc(xp_ready, 1)

                def add_up(self, n, l, c):
                    dve.wait_ge(m1_filled, n + 1).then_inc(stood["dve"], 1)
                    ps = M1[:P, 0:ST * F].rearrange("p (t f) -> p t f", f=F)
                    y, xx = Y[:, ST * c:ST * (c + 1), :], X[:, ST * c:ST * (c + 1), :]
                    if l < 2:
                        ins = nc.vector.tensor_tensor(y, ps, xx, ALU.add)
                    else:
                        ins = nc.vector.scalar_tensor_tensor(out=y, in0=ps, scalar=0.5, in1=xx, op0=ALU.is_gt, op1=ALU.add)
                    ins.then_inc(m1_read, 1)
                    dve.wait_ge(m1_read, n + 2).then_inc(stood["dve"], 1)
                    cols = [P, ST, F]
                    if l == 0 and c == 0:
                        dve.wait_ge(rden_ok, self.b + 1).then_inc(stood["dve"], 1)
                    if l == 0:
                        r = RDEN[:, ST * c:ST * (c + 1)].unsqueeze(2).to_broadcast(cols)
                        self.link(lambda: nc.vector.tensor_tensor(y, y, r, ALU.mult))
                        self.link(lambda: nc.vector.tensor_tensor(y, y, xx, ALU.add))
                    if l == 1:
                        self.link(lambda: nc.vector.tensor_tensor(y, y, B2[:, :].unsqueeze(1).to_broadcast(cols), ALU.add))

            def graph(b, kind):
                tasks = tasks_of(b, kind)
                at = dict(tasks)
                lay = Layers(b) if kind != "first" else None
                for j in range(TPG):
                    if kind != "last":
                        mask(b, j + 1, 0)
                        row_max(b, j)
                    if lay:
                        lay.at(j, 0)
                    if kind != "last":
                        mask(b, j + 1, 1)
                        shift(b, j)
                    if lay:
                        lay.at(j, 1)
                    if kind != "last":
                        mask(b, j + 1, 2)
                    unit = unit_of(b, kind, j // ST - 2) if j % ST == 1 else None
                    if unit:
                        keep(*unit)
                    task = at.get(j - 1)
                    if j == 0 and kind == "full":
                        n = (b - 1) * len(FULL) + (len(PRE) + len(FIRST)) - 1
                        keep_adj(n, ATN - 1)
                    elif j == 0 and kind == "last":
                        keep_adj((b - 1) * len(FULL) + (len(PRE) + len(FIRST)) - 1, ATN - 1)
                    if task and task[0] == "AT":
                        keep_adj(task_number(b, tasks, task), task[1])
                    if task and task[0] == "W":
                        lay.add_up(task_number(b, tasks, task), task[1], task[2])
                    task = at.get(j - 2)
                    if task and task[0] == "FT":
                        rest(b * 3 + 3 + task[1] + 1, task[1])
                    task = at.get(j - 4)
                    if task and task[0] == "FT":
                        low(b * 3 + 3 + task[1] + 1, task[1])
                    if lay:
                        lay.at(j, 2)
                    if kind != "last":
                        if j == DEGREES_AT:
                            degrees(b)
                        leaky(b, j)
                if lay:
                    assert lay.n == LINKS, lay.n

            for c in range(3):
                rest(c + 1, c)
                low(c + 1, c)
            for c in range(3):
                mask(0, 0, c)
            graph(0, "first")
            with dve.Fori(1, B) as b:
                graph(b, "full")
            graph(B, "last")


_INS = ['x', 'adj', 'L0_gnn_kernel', 'L0_gnn_attention_kernel', 'L0_gnn_attention_kernel_2', 'L0_gnn_bias',
        'L2_gnn_weight', 'L2_gnn_bias']


def kernel(**inputs):
    import numpy as _np
    import concourse.bacc as _bacc
    from concourse import mybir as _mybir
    from concourse.bass_utils import run_bass_kernel_spmd as _run

    nc = _bacc.Bacc("TRN2", target_bir_lowering=False, num_devices=1)
    arrays, args = {}, []
    for name in _INS:
        a = _np.ascontiguousarray(inputs[name])
        arrays[f"in_{name}_dram"] = a
        args.append(nc.dram_tensor(f"in_{name}_dram", a.shape, _mybir.dt.from_np(a.dtype), kind="ExternalInput").ap())
    out = nc.dram_tensor("out_0_dram", (B, N, F), _mybir.dt.float32, kind="ExternalOutput").ap()
    adj_resnorm(nc, *args, out)
    r = _run(nc, [arrays], core_ids=[0])
    return r.results[0]["out_0_dram"]
```

```python
import concourse.bass as bass
from concourse import mybir
from contextlib import ExitStack

B, N, F = 8, 1500, 64
H, D = 4, 16
P = 125
NT = N // P
ST = 4
NS = NT // ST
C = ST * P
NG = B * NS
TPS = H * ST
TPG = NS * TPS
UPG = NS * H
RS, LS, NGS = 3, 3, 6
VW = 32
TERMS = [(0, 0), (0, 1), (0, 2), (1, 0), (1, 1), (2, 0)]
KS = len(TERMS) * D
BIG = 2.0 ** 30
FLOOR = -1.0e8
EPS = 1e-5


CONSTS = 14

LINKS = 5 + 4 * 3
LAYER_AT = [(11, 0), (23, 1), (37, 2)]
AT0, ATN = 43, 5
DEGREES_AT = 37
NORMS_AT = (7, 18, 29, 43)
PLACES = {(5, 2): "sums", (6, 0): "reciprocal", (6, 1): "divide", (6, 2): "bias", (7, 0): "residual",
          (10, 0): ("scale", 0), (11, 2): ("x_low", 0), (21, 2): ("scale", 1), (23, 0): ("x_low", 1),
          (33, 2): ("scale", 2), (35, 0): ("x_low", 2), (47, 2): ("scale", 3)}
for norm_at in NORMS_AT:
    PLACES.update({(norm_at, 2): "mean", (norm_at + 1, 0): "centre", (norm_at + 2, 0): "add_squares",
                   (norm_at + 2, 1): "variance"})
X_HIGH = [10, 22, 34]
NARROW_AT = [7, 22, 44]
PREPARES = [(0, 1), (1, 1)]
POWERS = [(0, 1), (0, 3), (1, 3), (2, 2)]
MASKED_BY_DVE = {12, 13, 14, 15, 16, 19, 24, 26, 27, 28, 30, 31, 38, 39, 40, 41, 42, 44}


def masked_by_pe(j):
    return j not in MASKED_BY_DVE


def adj_resnorm(nc, x, adj, wv, wself, wother, bias0, w2, bias2, out):
    f32, bf16, f16, f8 = mybir.dt.float32, mybir.dt.bfloat16, mybir.dt.float16, mybir.dt.float8e4
    ALU, ACT, AX = mybir.AluOpType, mybir.ActivationFunctionType, mybir.AxisListType

    x_v = x.rearrange("b (s i k) f -> b i s k f", i=P, k=ST)
    out_v = out.rearrange("b (s i k) f -> b i s k f", i=P, k=ST)
    adj_v = adj.rearrange("b (s i k) m -> b s k i m", i=P, k=ST)

    ctx = ExitStack()
    with ctx:
        def sb(name, shape, dt):
            return ctx.enter_context(nc.sbuf_tensor(name, shape, dt))

        def sem(name):
            return ctx.enter_context(nc.semaphore(name))

        A = sb("A", [P, ST, N], bf16)
        A8 = sb("A8", [P, NT, N], f8)
        NEG = sb("NEG", [P, NGS, N], bf16)
        AT = sb("AT", [P, NS, N, ST], f8)
        FS = sb("FS", [KS, H, C], bf16)
        FO = sb("FO", [KS, H, N], bf16)
        R = sb("R", [P, RS, N], f32)
        L = sb("L", [P, LS, N], f32)
        PT = sb("PT", [P, 2, NT, C], f32)
        V = sb("V", [P, NT, H, D + 1], f32)
        VN = sb("VN", [P, NT, H, D], f32)
        XT = sb("XT", [F, C], f32)
        PARTS = sb("PARTS", [128, 3, N], bf16)
        REST = sb("REST", [128, C], f32)
        YT = sb("YT", [128, C], f32)
        O4 = sb("O4", [128, C], f32)
        OS = sb("OS", [P, NT, H, D + 1], f32)
        XIN = sb("XIN", [P, NT, F], f32)
        X = sb("X", [P, NT, F], f32)
        Y = sb("Y", [P, NT, F], f32)
        XP = sb("XP", [P, NT, 2 * F], f16)
        SQ = XP[:, :, :].rearrange("p t f -> p (t f)").bitcast(f32).rearrange("p (t f) -> p t f", f=F)
        DEG = sb("DEG", [P, NT], f32)
        RDEN = sb("RDEN", [P, NT], f32)
        RDEN1 = sb("RDEN1", [P, NT], f32)
        RSUM = sb("RSUM", [P, NT, H], f32)
        MEAN = sb("MEAN", [P, NT], f32)
        RSTD = sb("RSTD", [P, NT], f32)
        CMAX = sb("CMAX", [P, 4, 3], f32)
        RMAX = sb("RMAX", [P, 4], f32)
        SHIFT = sb("SHIFT", [P, 4], f32)
        WV = sb("WV", [F, H, D], f32)
        WA = sb("WA", [F, 2, H, D], f32)
        WW = sb("WW", [128, 2, F], f32)
        B0 = sb("B0", [P, F], f32)
        B2 = sb("B2", [P, F], f32)
        ID = sb("ID", [128, 128], f32)
        IDB = sb("IDB", [128, 128], bf16)
        E4 = sb("E4", [128, D + 1], f32)
        NHALF = sb("NHALF", [P, NT], f32)

        SP_ = ctx.enter_context(nc.psum_tensor("SP_", [128, 3, 512], f32))
        TP = ctx.enter_context(nc.psum_tensor("TP", [128, 3, 512], f32))
        M0 = ctx.enter_context(nc.psum_tensor("M0", [128, 512], f32))
        M1 = ctx.enter_context(nc.psum_tensor("M1", [128, 512], f32))

        weights_in = sem("weights_in")
        const_ok = sem("const_ok")
        x_in = sem("x_in")
        a_in = [sem(f"a_in{k}") for k in range(ST)]
        fs_in = [sem(f"fs_in{h}") for h in range(H)]
        fo_in = [sem(f"fo_in{h}") for h in range(H)]
        a8_ready = sem("a8_ready")
        neg_ready = sem("neg_ready")
        scores = sem("scores")
        relus = sem("relus")
        bank_free = sem("bank_free")
        rmax_ok = sem("rmax_ok")
        shift_ok = sem("shift_ok")
        l_ready = sem("l_ready")
        turned = sem("turned")
        exps = sem("exps")
        v_ready = sem("v_ready")
        pv_done = sem("pv_done")
        o4_ready = sem("o4_ready")
        ot_done = sem("ot_done")
        os_kept = sem("os_kept")
        m1_filled = sem("m1_filled")
        m1_read = sem("m1_read")
        hi_ready = sem("hi_ready")
        mid_ready = sem("mid_ready")
        lo_ready = sem("lo_ready")
        dve_seq = sem("dve_seq")
        deg_ok = sem("deg_ok")
        rden_ok = sem("rden_ok")
        squared = sem("squared")
        var_ok = sem("var_ok")
        rstd_ok = sem("rstd_ok")
        y_ready = sem("y_ready")
        x_ready = sem("x_ready")
        xh_ready = sem("xh_ready")
        xp_ready = sem("xp_ready")
        stored = sem("stored")
        pre_x = sem("pre_x")
        pre_xt = sem("pre_xt")
        pre_f = sem("pre_f")
        pre_fe = sem("pre_fe")
        pre_v = sem("pre_v")
        first_neg = sem("first_neg")
        pre_rest = sem("pre_rest")
        end_seq = sem("end_seq")
        end_var = sem("end_var")
        end_rstd = sem("end_rstd")
        end_x = sem("end_x")
        end_high = sem("end_high")
        end_low = sem("end_low")
        end_base = sem("end_base")
        end_y = sem("end_y")
        end_taken = sem("end_taken")
        end_back = sem("end_back")
        end_added = sem("end_added")
        stood = {e: sem(f"stood_{e}") for e in ("pe", "act", "dve", "pool")}
        block = ctx.enter_context(nc.Block())

        LATE = [(t - ATN, ("AT", t)) for t in range(ATN, NT)]
        LAYERS = [(at + 2 * c + d, (kind, l, c)) for at, l in LAYER_AT for c in range(3) for d, kind in enumerate("YW")]
        NEXT = [(18, ("XT", 0)), (19, ("FE", 0)), (20, ("FT", 0)), (29, ("XT", 1)), (30, ("FE", 1)), (31, ("FT", 1)),
                (33, ("XT", 2)), (34, ("FE", 2)), (35, ("FT", 2))]
        EARLY = [(AT0 + t, ("AT", t)) for t in range(ATN)]
        FULL = sorted(LATE + LAYERS + NEXT + EARLY)
        FIRST = sorted(NEXT + EARLY)
        LAST = LATE
        assert len({at for at, _ in FULL}) == len(FULL) and FULL[-1][0] == TPG - 1

        def task_number(b, tasks, task):
            n = [x for _, x in tasks].index(task)
            if tasks is FIRST:
                return n
            return (b - 1) * len(FULL) + len(FIRST) + n

        def tasks_of(kind):
            return {"first": FIRST, "full": FULL, "last": LAST}[kind]

        def unit_of(b, kind, u):
            if u >= 0:
                return (b, u) if kind != "last" else None
            return (b - 1, UPG + u) if kind != "first" else None

        NF = len(TERMS)

        @block.sync
        def _(sp):
            def load_parts(dst, sem_, side, h, cols):
                for n, pair in enumerate(TERMS):
                    sp.dma_start(dst[n * D:(n + 1) * D],
                                 PARTS[side * F + h * D:side * F + (h + 1) * D, pair[side], cols]).then_inc(sem_, 16)

            def load_x(dst, b, sem_):
                sp.dma_start(dst[:, :, :].rearrange("p (s k) f -> p s k f", k=ST), x_v[b]).then_inc(sem_, 16)

            def store(b):
                sp.wait_ge(x_ready, b * 4 + 4)
                sp.dma_start(out_v[b], X[:, :, :].rearrange("p (s k) f -> p s k f", k=ST)).then_inc(stored, 16)

            def graph(b, layers):
                for s in range(NS):
                    for h in range(H):
                        sp.wait_ge(scores, b * (3 * TPG) + 3 * (s * TPS + ST * h + ST))
                        if s == NS - 1:
                            if h == 0:
                                sp.wait_ge(lo_ready, b * 3 + 6)
                            load_parts(FO[:, h, :], fo_in[h], 1, h, slice(0, N))
                        sn = (s + 1) % NS
                        load_parts(FS[:, h, :], fs_in[h], 0, h, slice(sn * C, (sn + 1) * C))
                        if s == NS - 1 and h == 0:
                            load_x(XIN, b, x_in)
                        if layers and s == 0 and h == 0:
                            sp.wait_ge(dve_seq, (b - 1) * LINKS + 5)
                            load_x(XIN, (b + 1) % B, x_in)
                if layers:
                    store(b - 1)

            sp.sem_inc(stored, 16)
            load_x(XIN, 0, x_in)
            sp.dma_start(WV[:, :, :], wv.rearrange("h f o -> f h o")).then_inc(weights_in, 16)
            sp.dma_start(WA[:, 0, :, :], wself.rearrange("h f o -> f h o")).then_inc(weights_in, 16)
            sp.dma_start(WA[:, 1, :, :], wother.rearrange("h f o -> f h o")).then_inc(weights_in, 16)
            sp.dma_start(WW[0:F, 1, :], w2).then_inc(weights_in, 16)
            sp.dma_start(WW[F:2 * F, 1, :], w2).then_inc(weights_in, 16)
            sp.dma_start(B0[:, :], bias0.rearrange("a b h o -> (a b h o)").partition_broadcast(P)).then_inc(weights_in, 16)
            sp.dma_start(B2[:, :], bias2.partition_broadcast(P)).then_inc(weights_in, 16)
            sp.wait_ge(lo_ready, 1)
            load_parts(FS[:, 0, :], fs_in[0], 0, 0, slice(0, C))
            sp.wait_ge(lo_ready, NS)
            for h in range(H):
                load_parts(FO[:, h, :], fo_in[h], 1, h, slice(0, N))
                if h:
                    load_parts(FS[:, h, :], fs_in[h], 0, h, slice(0, C))
            load_x(XIN, 1, x_in)
            graph(0, False)
            with sp.Fori(1, B) as b:
                graph(b, True)
            for c in range(NS):
                sp.wait_ge(end_x, 9 + c + 1)
                sp.dma_start(out_v[B - 1][:, c], X[:, ST * c:ST * (c + 1), :]).then_inc(stored, 16)
            for h in range(H):
                sp.wait_ge(fs_in[h], 16 * NF * (NG + 1))
                sp.wait_ge(fo_in[h], 16 * NF * (B + 1))
            sp.wait_ge(x_in, 16 * (2 * B + 1))
            sp.wait_ge(stored, 16 * B + 16 * NS)

        @block.gpsimd
        def _(pool):
            made = [0]

            def const(ins):
                ins.then_inc(const_ok, 1)
                made[0] += 1
                pool.wait_ge(const_ok, made[0])

            for t in (ID, IDB, E4):
                const(nc.gpsimd.memset(t[:, :], 0.0))
            const(nc.gpsimd.memset(WW[:, 0, :], 0.0))
            const(nc.gpsimd.memset(NHALF[:, :], -0.5))
            const(nc.gpsimd.memset(V[:, :, :, D:D + 1], 1.0))

            def ones(ap, base, cols):
                const(nc.gpsimd.affine_select(out=ap, in_=ap, compare_op=ALU.not_equal, fill=1.0, base=-base,
                                              pattern=[[-1, cols]], channel_multiplier=1))

            ones(ID[:, :], 0, 128)
            ones(IDB[:, :], 0, 128)
            for c in range(4):
                ones(E4[:, :], VW * c, D + 1)
            for c in range(2):
                ones(WW[:, 0, :], F * c, F)
            assert made[0] == CONSTS

            def load(b, s, k):
                pool.dma_start(A[:, k, :], adj_v[b, s, k]).then_inc(a_in[k], 16)

            def negate(t, k, done=neg_ready):
                nc.gpsimd.tensor_scalar(NEG[:, t % NGS, :].rearrange("p (s k i) -> p s i k", k=ST, i=P),
                                        A[:, k, :].rearrange("p (s i k) -> p s i k", i=P, k=ST),
                                        -1.0, BIG, ALU.add, ALU.mult).then_inc(done, 1)

            def power(n):
                pool.wait_ge(var_ok, n + 1)
                nc.gpsimd.tensor_tensor(RSTD[:, :], RSTD[:, :], NHALF[:, :], ALU.pow).then_inc(rstd_ok, 1)

            def prepare(b, l):
                pool.wait_ge(x_ready, b * 4 + l + 1)
                if l == 0:
                    nc.gpsimd.tensor_tensor(Y[:, :, :], X[:, :, :], RDEN1[:, :].unsqueeze(2).to_broadcast([P, NT, F]),
                                            ALU.mult).then_inc(y_ready, 1)
                else:
                    nc.gpsimd.tensor_tensor(Y[:, :, :], X[:, :, :], B2[:, :].unsqueeze(1).to_broadcast([P, NT, F]),
                                            ALU.add).then_inc(y_ready, 1)

            def graph(b, layers):
                for s in range(NS):
                    g = b * NS + s
                    t0 = (s + 1) % NS * ST
                    for k in range(ST):
                        pool.wait_ge(a8_ready, g * ST + k + 1)
                        pool.wait_ge(neg_ready, g * ST + k + 1)
                        load(b if s + 1 < NS else (b + 1) % B, (s + 1) % NS, k)
                    for k in range(ST):
                        if k >= 2:
                            pool.wait_ge(bank_free, b * (3 * TPG) + 3 * (s * TPS + TPS - ST + k - 2) + 3 + 3)
                        elif layers or s > 0:
                            pool.wait_ge(bank_free, b * (3 * TPG) + 3 * (s * TPS - ST + k + 2) + 3 + 3)
                        pool.wait_ge(a_in[k], g * 16 + 32).then_inc(stood["pool"], 1)
                        negate(t0 + k, k)
                        for n, place in enumerate(POWERS):
                            if layers and place == (s, k):
                                power((b - 1) * 4 + n)
                        if layers and (s, k) in PREPARES:
                            prepare(b - 1, PREPARES.index((s, k)))

            pool.wait_ge(weights_in, 7 * 16)
            for k in range(ST):
                load(0, 0, k)
            pool.wait_ge(a_in[0], 16)
            negate(0, 0, first_neg)
            pool.wait_ge(first_neg, ST)
            pool.sem_inc(neg_ready, ST)
            graph(0, False)
            with pool.Fori(1, B) as b:
                graph(b, True)
            def end_power(l, c):
                part = RSTD[:, ST * c:ST * (c + 1)]
                pool.wait_ge(end_var, 3 * l + c + 1)
                nc.gpsimd.tensor_tensor(part, part, NHALF[:, 0:ST], ALU.pow).then_inc(end_rstd, 1)

            def end_prepare(l, c):
                pool.wait_ge(end_x, 3 * l + c + 1)
                rows, cols = slice(ST * c, ST * (c + 1)), [P, ST, F]
                if l == 0:
                    factor, op = RDEN1[:, rows].unsqueeze(2).to_broadcast(cols), ALU.mult
                else:
                    factor, op = B2[:, :].unsqueeze(1).to_broadcast(cols), ALU.add
                nc.gpsimd.tensor_tensor(Y[:, rows, :], X[:, rows, :], factor, op).then_inc(end_base, 1)

            for l in range(4):
                for c in range(NS):
                    end_power(l, c)
                    if c and l < 2:
                        end_prepare(l, c - 1)
                if l < 2:
                    end_prepare(l, NS - 1)
            for k in range(ST):
                pool.wait_ge(a_in[k], 16 * (NG + 1))

        @block.tensor
        def _(pe):
            pe.wait_ge(weights_in, 7 * 16)
            pe.wait_ge(const_ok, CONSTS)

            def score(b, j, c):
                s, i = divmod(j % TPG, TPS)
                h, k = divmod(i, ST)
                g = b * NS + j // TPS
                if k == 0 and c == 0:
                    pe.wait_ge(fs_in[h], g * (16 * NF) + 16 * NF)
                    if s == 0:
                        pe.wait_ge(fo_in[h], b * (16 * NF) + 16 * NF * (j // TPG + 1))
                pe_mask = masked_by_pe(j % TPG)
                if c == 0 and pe_mask:
                    pe.wait_ge(neg_ready, g * ST + k + 1)
                pe.wait_ge(bank_free, b * (3 * TPG) + 3 * j + c + 1)
                ins = nc.tensor.matmul(SP_[:P, c, 0:C], FS[:, h, k * P:(k + 1) * P], FO[:, h, c * C:(c + 1) * C],
                                       start=True, stop=not pe_mask)
                if pe_mask:
                    ins = nc.tensor.matmul(SP_[:P, c, 0:C], IDB[:P, :P],
                                           NEG[:, (s * ST + k) % NGS, c * C:(c + 1) * C], start=False, stop=True)
                ins.then_inc(scores, 1)

            def turn(b, j, half):
                if half == 0:
                    pe.wait_ge(l_ready, b * TPG + j + 1 + RS)
                    pe.wait_ge(exps, b * TPG + j + 1)
                for m in range(half * NT // 2, (half + 1) * NT // 2):
                    last = nc.tensor.transpose(TP[:P, m // 4, m % 4 * P:(m % 4 + 1) * P],
                                               L[:, j % LS, m * P:(m + 1) * P], ID[:P, :P])
                if half == 1:
                    last.then_inc(turned, 1)

            def weigh(b, u, r):
                h = u % H
                if r == 0:
                    pe.wait_ge(exps, b * TPG + ST * u + ST + 1)
                    pe.wait_ge(os_kept, b * UPG + u + 1)
                    if u == 0:
                        pe.wait_ge(v_ready, b + 1)
                for c in range(4):
                    last = nc.tensor.matmul(M0[VW * c:VW * c + D + 1, 0:C], V[:, 3 * c + r, h, :],
                                            PT[:, h % 2, 3 * c + r, :], start=(r == 0), stop=(r == 2))
                if r == 2:
                    last.then_inc(pv_done, 1)

            def gather(b, u):
                pe.wait_ge(o4_ready, b * UPG + u + 1)
                for k in range(ST):
                    last = nc.tensor.matmul(M0[:P, k * VW:k * VW + D + 1], O4[:, k * P:(k + 1) * P], E4[:, :],
                                            start=True, stop=True)
                last.then_inc(ot_done, 1)

            def collect(c, m0, m1):
                for m in range(m0, m1):
                    last = nc.tensor.matmul(M1[:, 0:C], XP[:, m, :], AT[:, m // ST, c * C:(c + 1) * C, m % ST],
                                            start=(m == 0), stop=(m == NT - 1))
                return last

            def m1_task(b, n, task):
                if task[0] == "AT":
                    t = task[1]
                    pe.wait_ge(rden_ok, (b if t < ATN else b - 1) + 1)
                elif task[0] == "Y":
                    pe.wait_ge(xp_ready, (b - 1) * 3 + task[1] + 1)
                    pe.wait_ge(m1_read, n + 1).then_inc(stood["pe"], 1)
                    collect(task[-1], 0, 6)
                    return
                elif task[0] == "XT":
                    pe.wait_ge(x_in, b * 32 + 32)
                pe.wait_ge(m1_read, n + 1).then_inc(stood["pe"], 1)
                fill_m1(task).then_inc(m1_filled, 1)

            def fill_m1(task, bank=M1, xt=XT):
                kind, c = task[0], task[-1]
                if kind == "AT":
                    words = A8[:, c, :].bitcast(f32)
                    for q in range(NS):
                        last = nc.tensor.transpose(bank[:P, q * P:(q + 1) * P], words[:, q * P:(q + 1) * P], ID[:P, :P])
                elif kind == "W":
                    for k in range(ST):
                        last = nc.tensor.matmul(bank[:P, k * F:(k + 1) * F], YT[:, k * P:(k + 1) * P],
                                                WW[:, 1 if task[1] == 1 else 0, :], start=True, stop=True)
                elif kind == "XT":
                    for k in range(ST):
                        last = nc.tensor.transpose(bank[:F, k * P:(k + 1) * P], XIN[:, ST * c + k, :], ID[:P, :P])
                elif kind == "FE":
                    for k in range(ST):
                        last = nc.tensor.matmul(bank[:P, k * F:(k + 1) * F], xt[:F, k * P:(k + 1) * P],
                                                WV[:, :, :].rearrange("f h o -> f (h o)"), start=True, stop=True)
                else:
                    last = nc.tensor.matmul(bank[:, 0:C], WA[:, :, :, :].rearrange("f s h o -> f (s h o)"), xt[:F, 0:C],
                                            start=True, stop=True)
                return last

            pe.wait_ge(x_in, 16)
            pre_xts = (XT, YT, O4)
            for c in range(NS):
                fill_m1(("XT", c), SP_[:, c]).then_inc(pre_x, 1)
            for c in range(NS):
                pe.wait_ge(pre_xt, c + 1)
                fill_m1(("FT", c), TP[:, c], pre_xts[c]).then_inc(pre_f, 1)
                fill_m1(("FE", c), SP_[:, c], pre_xts[c]).then_inc(pre_fe, 1)
            pe.wait_ge(pre_v, NS)
            for j in range(2):
                for c in range(3):
                    score(0, j, c)

            def graph(b, kind):
                tasks = tasks_of(kind)
                at = dict(tasks)
                for j in range(TPG):
                    back = (b, j - 1) if j else (b - 1, TPG - 1)
                    turns = (kind != "first" or j) and (kind != "last" or j == 0)
                    for c in range(3):
                        if kind != "last":
                            score(b, j + 2, c)
                        before = at.get(j - 1)
                        if c < 2 and before and before[0] == "Y":
                            last = collect(before[-1], 6 + 3 * c, 9 + 3 * c)
                            if c == 1:
                                last.then_inc(m1_filled, 1)
                        if turns and c < 2:
                            turn(*back, c)
                    if j % ST:
                        unit = unit_of(b, kind, (j - 1) // ST - 1)
                        if unit:
                            weigh(*unit, j % ST - 1)
                    else:
                        unit = unit_of(b, kind, j // ST - 2)
                        if unit:
                            gather(*unit)
                    if j in at:
                        m1_task(b, task_number(b, tasks, at[j]), at[j])

            graph(0, "first")
            with pe.Fori(1, B) as b:
                graph(b, "full")
            graph(B, "last")

            pe.wait_ge(m1_read, len(FIRST) + (B - 1) * len(FULL) + len(LAST) + 1)
            pe.wait_ge(relus, B * (3 * TPG) + 6)
            pe.wait_ge(bank_free, B * (3 * TPG) + 3 + 3)
            pe.wait_ge(exps, B * TPG + 1)
            parts = (YT, O4, REST)
            for l in range(3):
                for q in range(NS):
                    pe.wait_ge(end_low, 3 * l + q + 1)
                    for c in range(NS):
                        if l and q == 0:
                            pe.wait_ge(end_taken, 3 * (l - 1) + c + 1)
                        for m in range(ST * q, ST * (q + 1)):
                            last = nc.tensor.matmul(SP_[:, c, 0:C], XP[:, m, :], AT[:, q, c * C:(c + 1) * C, m % ST],
                                                    start=(m == 0), stop=(m == NT - 1))
                        if q == NS - 1:
                            last.then_inc(end_y, 1)
                for c in range(NS):
                    if l:
                        pe.wait_ge(end_added, 3 * (l - 1) + c + 1)
                    pe.wait_ge(end_taken, 3 * l + c + 1)
                    for k in range(ST):
                        last = nc.tensor.matmul(TP[:P, c, k * F:(k + 1) * F], parts[c][:, k * P:(k + 1) * P],
                                                WW[:, 1 if l == 1 else 0, :], start=True, stop=True)
                    last.then_inc(end_back, 1)

        @block.scalar
        def _(act):
            def relu(b, j, c):
                if c == 0:
                    act.wait_ge(l_ready, b * TPG + j + 1)
                act.wait_ge(scores, b * (3 * TPG) + 3 * j + c + 1)
                nc.scalar.activation(R[:, j % RS, c * C:(c + 1) * C], SP_[:P, c, 0:C], ACT.Relu,
                                     scale=4.0).then_inc(relus, 1)

            def expo(b, j):
                h, k = j // ST % H, j % ST
                act.wait_ge(turned, b * TPG + j + 1 + LS)
                nc.scalar.activation(PT[:, h % 2, :, k * P:(k + 1) * P].rearrange("p (a m) n -> p a m n", a=3),
                                     TP[:P, :, 0:C].rearrange("p a (m n) -> p a m n", m=4), ACT.Exp,
                                     scale=0.05).then_inc(exps, 1)

            def take(b, u):
                act.wait_ge(pv_done, b * UPG + u + 1)
                nc.scalar.activation(O4[:, :], M0[:, 0:C], ACT.Copy).then_inc(o4_ready, 1)

            def narrow(b, g, t):
                act.wait_ge(a_in[t % ST], g * 16 + 16).then_inc(stood["act"], 1)
                nc.scalar.activation(A8[:, t, :], A[:, t % ST, :], ACT.Copy, accum_out=DEG[:, t:t + 1],
                                     saturate=False).then_inc(a8_ready, 1)

            def values(b):
                nc.scalar.activation(V[:, :, :, 0:D], VN[:, :, :, :], ACT.Copy).then_inc(v_ready, 1)

            def read_m1(n, task):
                kind, c = task[0], task[-1]
                act.wait_ge(m1_filled, n + 1)
                if kind == "XT":
                    ins = nc.scalar.activation(XT[:, :], M1[:F, 0:C], ACT.Copy)
                elif kind == "FE":
                    ins = nc.scalar.activation(VN[:, ST * c:ST * (c + 1), :, :],
                                               M1[:P, 0:ST * F].rearrange("p (t h o) -> p t h o", h=H, o=D), ACT.Copy)
                else:
                    ins = nc.scalar.activation(YT[:, :], M1[:, 0:C], ACT.Copy)
                ins.then_inc(m1_read, 1)

            def high(n, c):
                act.wait_ge(m1_filled, n + 1)
                nc.scalar.activation(PARTS[:, 0, c * C:(c + 1) * C], M1[:, 0:C], ACT.Copy).then_inc(hi_ready, 1)

            def middle(n, c):
                act.wait_ge(m1_read, n + 2)
                nc.scalar.activation(PARTS[:, 1, c * C:(c + 1) * C], REST[:, :], ACT.Copy).then_inc(mid_ready, 1)

            def graph(b, kind):
                tasks = tasks_of(kind)
                at = dict(tasks)
                for j in range(TPG):
                    unit = unit_of(b, kind, j // ST - 2) if j % ST == 0 else None
                    if unit:
                        take(*unit)
                    task = at.get(j - 1)
                    if task and task[0] in ("XT", "FE"):
                        read_m1(task_number(b, tasks, task), task)
                    if task and task[0] == "FT":
                        if task[1] == NS - 1:
                            for h in (2, 3):
                                act.wait_ge(fs_in[h], b * (NS * 16 * NF) + NS * 16 * NF)
                        high(task_number(b, tasks, task), task[1])
                    task = at.get(j - 3)
                    if task and task[0] == "FT":
                        middle(task_number(b, tasks, task), task[1])
                    if j in X_HIGH and kind == "full":
                        act.wait_ge(x_ready, (b - 1) * 4 + X_HIGH.index(j) + 1)
                        nc.scalar.activation(XP[:, :, 0:F], X[:, :, :], ACT.Copy).then_inc(xh_ready, 1)
                    if kind != "last" and j == ST:
                        if kind == "first":
                            act.wait_ge(pre_v, NS)
                        else:
                            act.wait_ge(m1_read, task_number(b, tasks, LATE[0][1]) + 1)
                        values(b)
                    if kind != "last":
                        relu(b, j + 2, 0)
                        relu(b, j + 2, 1)
                    task = at.get(j - 1)
                    if task and task[0] == "Y":
                        read_m1(task_number(b, tasks, task), task)
                    if j - 1 in NORMS_AT and kind == "full":
                        l = NORMS_AT.index(j - 1)
                        act.wait_ge(dve_seq, (b - 1) * LINKS + 5 + 3 * l + 2)
                        nc.scalar.activation(SQ, Y[:, :, :], ACT.Square).then_inc(squared, 1)
                    if (kind != "first" or j) and (kind != "last" or j == 0):
                        expo(b, j - 1) if j else expo(b - 1, TPG - 1)
                    if kind != "last":
                        relu(b, j + 2, 2)
                        if 0 <= j - NARROW_AT[j // TPS] < ST:
                            t = (j // TPS + 1) % NS * ST + j - NARROW_AT[j // TPS]
                            if j // TPS == NS - 1:
                                act.wait_ge(rden_ok, b + 1)
                                act.wait_ge(m1_filled, task_number(b, tasks, ("AT", t)) + 1)
                            narrow(b, b * NS + j // TPS + 1, t)

            for c, xt in enumerate((XT, YT, O4)):
                act.wait_ge(pre_x, c + 1)
                nc.scalar.activation(xt[:F, :], SP_[:F, c, 0:C], ACT.Copy).then_inc(pre_xt, 1)
            for c in range(NS):
                act.wait_ge(pre_f, c + 1)
                nc.scalar.activation(PARTS[:, 0, c * C:(c + 1) * C], TP[:, c, 0:C], ACT.Copy).then_inc(hi_ready, 1)
                act.wait_ge(pre_fe, c + 1)
                nc.scalar.activation(VN[:, ST * c:ST * (c + 1), :, :],
                                     SP_[:P, c, 0:ST * F].rearrange("p (t h o) -> p t h o", h=H, o=D),
                                     ACT.Copy).then_inc(pre_v, 1)
                act.wait_ge(pre_rest, c + 1)
                nc.scalar.activation(PARTS[:, 1, c * C:(c + 1) * C], REST[:, :], ACT.Copy).then_inc(mid_ready, 1)
            for t in range(ST):
                narrow(0, 0, t)
            for j in range(2):
                for c in range(3):
                    relu(0, j, c)
            graph(0, "first")
            with act.Fori(1, B) as b:
                graph(b, "full")
            graph(B, "last")

            parts = (YT, O4, REST)
            for l in range(3):
                for c in range(NS):
                    act.wait_ge(end_x, 3 * l + c + 1)
                    nc.scalar.activation(XP[:, ST * c:ST * (c + 1), 0:F], X[:, ST * c:ST * (c + 1), :],
                                         ACT.Copy).then_inc(end_high, 1)
                for c in range(NS):
                    act.wait_ge(end_y, 3 * l + c + 1)
                    nc.scalar.activation(parts[c][:, :], SP_[:, c, 0:C], ACT.Copy).then_inc(end_taken, 1)

        @block.vector
        def _(dve):
            dve.sem_inc(bank_free, 3)
            dve.sem_inc(l_ready, RS)
            dve.sem_inc(turned, LS)
            dve.sem_inc(exps, 1)
            dve.sem_inc(m1_read, 1)
            nc.vector.memset(M0[:, :], 0.0).then_inc(os_kept, 1)
            dve.wait_ge(weights_in, 7 * 16)
            dve.wait_ge(const_ok, CONSTS)

            def mask(b, j, c):
                s, i = divmod(j % TPG, TPS)
                h, k = divmod(i, ST)
                if c == 0:
                    dve.wait_ge(turned, b * TPG + j + 1)
                    if h == 0:
                        dve.wait_ge(neg_ready, (b * NS + j // TPS) * ST + k + 1)
                dve.wait_ge(relus, b * (3 * TPG) + 3 * j + c + 1).then_inc(stood["dve"], 1)
                if masked_by_pe(j % TPG):
                    in1 = R[:, j % RS, c * C:(c + 1) * C]
                else:
                    in1 = NEG[:, (s * ST + k) % NGS, c * C:(c + 1) * C]
                nc.vector.tensor_tensor_reduce(out=L[:, j % LS, c * C:(c + 1) * C], in0=SP_[:P, c, 0:C],
                                               in1=in1, scale=1.0, scalar=FLOOR, op0=ALU.add, op1=ALU.max,
                                               accum_out=CMAX[:, j % 4, c:c + 1]).then_inc(bank_free, 1)

            def row_max(b, j):
                dve.wait_ge(bank_free, b * (3 * TPG) + 3 * j + 3 + 3)
                nc.vector.tensor_reduce(RMAX[:, j % 4:j % 4 + 1], CMAX[:, j % 4, :], AX.X, ALU.max).then_inc(rmax_ok, 1)

            def shift(b, j):
                dve.wait_ge(rmax_ok, b * TPG + j + 1)
                m = RMAX[:, j % 4:j % 4 + 1]
                if masked_by_pe(j % TPG):
                    nc.vector.tensor_copy(SHIFT[:, j % 4:j % 4 + 1], m).then_inc(shift_ok, 1)
                else:
                    nc.vector.scalar_tensor_tensor(out=SHIFT[:, j % 4:j % 4 + 1], in0=m, scalar=5.0, in1=m,
                                                   op0=ALU.mult, op1=ALU.max).then_inc(shift_ok, 1)

            def leaky(b, j):
                dve.wait_ge(shift_ok, b * TPG + j + 1)
                row, m = L[:, j % LS, :], SHIFT[:, j % 4:j % 4 + 1]
                if masked_by_pe(j % TPG):
                    nc.vector.tensor_scalar(row, row, m, None, ALU.subtract).then_inc(l_ready, 1)
                else:
                    nc.vector.scalar_tensor_tensor(out=row, in0=row, scalar=m, in1=R[:, j % RS, :],
                                                   op0=ALU.subtract, op1=ALU.add).then_inc(l_ready, 1)

            def keep(b, u):
                s, h = divmod(u, H)
                dve.wait_ge(ot_done, b * UPG + u + 1)
                nc.vector.tensor_copy(OS[:, s * ST:(s + 1) * ST, h, :],
                                      M0[:P, 0:ST * VW].rearrange("p (k o) -> p k o", k=ST)[:, :, 0:D + 1]).then_inc(os_kept, 1)

            def keep_adj(n, t):
                dve.wait_ge(m1_filled, n + 1)
                words = AT[:, :, :, :].rearrange("p q n k -> p (q n k)").bitcast(f32).rearrange("p (q n) -> p q n", q=NS)
                nc.vector.tensor_copy(words[:, :, t * P:(t + 1) * P],
                                      M1[:P, 0:NS * P].rearrange("p (q n) -> p q n", q=NS)).then_inc(m1_read, 1)

            def rest(hi, c):
                dve.wait_ge(lo_ready, hi - 1)
                dve.wait_ge(hi_ready, hi)
                nc.vector.tensor_tensor(REST[:, :], M1[:, 0:C], PARTS[:, 0, c * C:(c + 1) * C],
                                        ALU.subtract).then_inc(m1_read, 1)

            def low(mid, c):
                dve.wait_ge(mid_ready, mid)
                nc.vector.tensor_tensor(PARTS[:, 2, c * C:(c + 1) * C], REST[:, :], PARTS[:, 1, c * C:(c + 1) * C],
                                        ALU.subtract).then_inc(lo_ready, 1)

            bc3 = [P, NT, F]
            y3, x3 = Y[:, :, :], X[:, :, :]

            def degrees(b):
                dve.wait_ge(a8_ready, b * NT + NT)
                nc.vector.tensor_scalar(DEG[:, :], DEG[:, :], 1.0, None, ALU.add).then_inc(deg_ok, 1)
                dve.wait_ge(deg_ok, 2 * b + 1)
                nc.vector.reciprocal(RDEN[:, :], DEG[:, :]).then_inc(deg_ok, 1)
                dve.wait_ge(deg_ok, 2 * b + 2)
                nc.vector.tensor_scalar(RDEN1[:, :], RDEN[:, :], 1.0, None, ALU.add).then_inc(rden_ok, 1)

            class Layers:

                def __init__(self, b):
                    self.base, self.b, self.n = (b - 1) * LINKS, b - 1, 0

                def at(self, j, place):
                    step = PLACES.get((j, place))
                    if step:
                        name, *l = step if isinstance(step, tuple) else (step,)
                        {"sums": self.sums, "reciprocal": self.reciprocal, "divide": self.divide, "bias": self.bias,
                         "residual": self.residual, "mean": self.mean, "centre": self.centre,
                         "add_squares": self.add_squares, "variance": self.variance, "scale": self.scale,
                         "x_low": self.x_low}[name](*l)

                def link(self, make):
                    if self.n:
                        dve.wait_ge(dve_seq, self.base + self.n).then_inc(stood["dve"], 1)
                    make().then_inc(dve_seq, 1)
                    self.n += 1

                def sums(self):
                    dve.wait_ge(os_kept, self.b * UPG + UPG + 1)
                    self.link(lambda: nc.vector.tensor_scalar(RSUM[:, :, :], OS[:, :, :, D], 1e-30, None, ALU.max))

                def reciprocal(self):
                    self.link(lambda: nc.vector.reciprocal(RSUM[:, :, :], RSUM[:, :, :]))

                def divide(self):
                    self.link(lambda: nc.vector.tensor_tensor(
                        y3.rearrange("p t (h o) -> p (t h) o", h=H), OS[:, :, :, 0:D].rearrange("p t h o -> p (t h) o"),
                        RSUM[:, :, :].rearrange("p t h -> p (t h)").unsqueeze(2).to_broadcast([P, NT * H, D]), ALU.mult))

                def bias(self):
                    self.link(lambda: nc.vector.tensor_tensor(y3, y3, B0[:, :].unsqueeze(1).to_broadcast(bc3), ALU.add))

                def residual(self):
                    dve.wait_ge(x_in, self.b * 32 + 48)
                    self.link(lambda: nc.vector.scalar_tensor_tensor(out=y3, in0=y3, scalar=0.0, in1=XIN[:, :, :],
                                                                     op0=ALU.max, op1=ALU.add))

                def mean(self):
                    self.link(lambda: nc.vector.tensor_reduce(MEAN[:, :], y3, AX.X, ALU.add))

                def centre(self):
                    self.link(lambda: nc.vector.scalar_tensor_tensor(
                        out=y3, in0=MEAN[:, :].unsqueeze(2).to_broadcast(bc3), scalar=-1.0 / F, in1=y3,
                        op0=ALU.mult, op1=ALU.add))

                def add_squares(self):
                    dve.wait_ge(squared, self.b * 4 + (self.n - 5) // 3 + 1)
                    self.link(lambda: nc.vector.tensor_reduce(RSTD[:, :], SQ, AX.X, ALU.add))

                def variance(self):
                    dve.wait_ge(dve_seq, self.base + self.n).then_inc(stood["dve"], 1)
                    nc.vector.tensor_scalar(RSTD[:, :], RSTD[:, :], 1.0 / F, EPS, ALU.mult, ALU.add).then_inc(var_ok, 1)

                def scale(self, l):
                    dve.wait_ge(rstd_ok, self.b * 4 + l + 1)
                    if l == 0:
                        dve.wait_ge(stored, self.b * 16 + 16)
                    nc.vector.tensor_tensor(x3, y3, RSTD[:, :].unsqueeze(2).to_broadcast(bc3), ALU.mult).then_inc(x_ready, 1)

                def x_low(self, l):
                    dve.wait_ge(xh_ready, self.b * 3 + l + 1)
                    nc.vector.tensor_tensor(XP[:, :, F:2 * F], x3, XP[:, :, 0:F], ALU.subtract).then_inc(xp_ready, 1)

                def add_up(self, n, l, c):
                    if l < 2 and c == 0:
                        dve.wait_ge(y_ready, self.b * 2 + l + 1)
                    dve.wait_ge(m1_filled, n + 1).then_inc(stood["dve"], 1)
                    ps = M1[:P, 0:ST * F].rearrange("p (t f) -> p t f", f=F)
                    y, xx = Y[:, ST * c:ST * (c + 1), :], X[:, ST * c:ST * (c + 1), :]
                    if l == 0:
                        for k in range(ST):
                            t = ST * c + k
                            ins = nc.vector.scalar_tensor_tensor(out=Y[:, t, :], in0=ps[:, k, :], scalar=RDEN[:, t:t + 1],
                                                                 in1=Y[:, t, :], op0=ALU.mult, op1=ALU.add)
                    elif l == 1:
                        ins = nc.vector.tensor_tensor(y, ps, y, ALU.add)
                    else:
                        ins = nc.vector.scalar_tensor_tensor(out=y, in0=ps, scalar=0.5, in1=xx, op0=ALU.is_gt, op1=ALU.add)
                    ins.then_inc(m1_read, 1)
                    if c == 2:
                        dve.wait_ge(m1_read, n + 2).then_inc(stood["dve"], 1)

            def graph(b, kind):
                tasks = tasks_of(kind)
                at = dict(tasks)
                lay = Layers(b) if kind == "full" else None
                for j in range(TPG):
                    if kind != "last":
                        mask(b, j + 1, 0)
                        row_max(b, j)
                    if lay:
                        lay.at(j, 0)
                    if kind != "last":
                        mask(b, j + 1, 1)
                        shift(b, j)
                    if lay:
                        lay.at(j, 1)
                    unit = unit_of(b, kind, j // ST - 2) if j % ST == 1 else None
                    if unit:
                        keep(*unit)
                    if kind != "last":
                        mask(b, j + 1, 2)
                    task = at.get(j - 1)
                    if j == 0 and kind != "first":
                        keep_adj((b - 1) * len(FULL) + len(FIRST) - 1, ATN - 1)
                    if task and task[0] == "AT":
                        keep_adj(task_number(b, tasks, task), task[1])
                    if task and task[0] == "W":
                        lay.add_up(task_number(b, tasks, task), task[1], task[2])
                    task = at.get(j - 2)
                    if task and task[0] == "FT":
                        rest(b * 3 + 3 + task[1] + 1, task[1])
                    task = at.get(j - 4)
                    if task and task[0] == "FT":
                        low(b * 3 + 3 + task[1] + 1, task[1])
                    if lay:
                        lay.at(j, 2)
                    if kind != "last":
                        if j == DEGREES_AT:
                            degrees(b)
                        leaky(b, j)
                if lay:
                    assert lay.n == LINKS, lay.n

            for c in range(NS):
                if c:
                    dve.wait_ge(lo_ready, c)
                dve.wait_ge(hi_ready, c + 1)
                nc.vector.tensor_tensor(REST[:, :], TP[:, c, 0:C], PARTS[:, 0, c * C:(c + 1) * C],
                                        ALU.subtract).then_inc(pre_rest, 1)
                low(c + 1, c)
            for k in range(1, ST):
                dve.wait_ge(a_in[k], 16)
                nc.vector.tensor_scalar(NEG[:, k, :].rearrange("p (s k i) -> p s i k", k=ST, i=P),
                                        A[:, k, :].rearrange("p (s i k) -> p s i k", i=P, k=ST),
                                        -1.0, BIG, ALU.add, ALU.mult).then_inc(first_neg, 1)
            for c in range(3):
                mask(0, 0, c)
            graph(0, "first")
            with dve.Fori(1, B) as b:
                graph(b, "full")
            graph(B, "last")

            count, of_chunk = [0], [0, 0, 0]

            def step(c, ins):
                ins.then_inc(end_seq, 1)
                count[0] += 1
                of_chunk[c] = count[0]

            def follow(c):
                dve.wait_ge(end_seq, of_chunk[c])

            def start(c):
                rows = slice(ST * c, ST * (c + 1))
                sums = RSUM[:, rows, :]
                heads = "p t (h o) -> p (t h) o"
                if c == 0:
                    dve.wait_ge(os_kept, B * UPG + 1)
                step(c, nc.vector.tensor_scalar(sums, OS[:, rows, :, D], 1e-30, None, ALU.max))
                follow(c)
                step(c, nc.vector.reciprocal(sums, sums))
                follow(c)
                step(c, nc.vector.tensor_tensor(
                    Y[:, rows, :].rearrange(heads, h=H), OS[:, rows, :, 0:D].rearrange("p t h o -> p (t h) o"),
                    sums.rearrange("p t h -> p (t h)").unsqueeze(2).to_broadcast([P, ST * H, D]), ALU.mult))
                follow(c)
                step(c, nc.vector.tensor_tensor(Y[:, rows, :], Y[:, rows, :], B0[:, :].unsqueeze(1).to_broadcast([P, ST, F]),
                                                ALU.add))
                if c == 0:
                    dve.wait_ge(x_in, 16 * (2 * B + 1))
                follow(c)
                step(c, nc.vector.scalar_tensor_tensor(out=Y[:, rows, :], in0=Y[:, rows, :], scalar=0.0,
                                                       in1=XIN[:, rows, :], op0=ALU.max, op1=ALU.add))

            def add(l, c):
                dve.wait_ge(end_back, 3 * l + c + 1)
                if l < 2:
                    dve.wait_ge(end_base, 3 * l + c + 1)
                y, ps = Y[:, ST * c:ST * (c + 1), :], TP[:P, c, 0:ST * F].rearrange("p (t f) -> p t f", f=F)
                if l == 0:
                    for k in range(ST):
                        t = ST * c + k
                        ins = nc.vector.scalar_tensor_tensor(out=Y[:, t, :], in0=ps[:, k, :], scalar=RDEN[:, t:t + 1],
                                                             in1=Y[:, t, :], op0=ALU.mult, op1=ALU.add)
                elif l == 1:
                    ins = nc.vector.tensor_tensor(y, ps, y, ALU.add)
                else:
                    ins = nc.vector.scalar_tensor_tensor(out=y, in0=ps, scalar=0.5, in1=X[:, ST * c:ST * (c + 1), :],
                                                         op0=ALU.is_gt, op1=ALU.add)
                ins.then_inc(end_added, 1)
                dve.wait_ge(end_added, 3 * l + c + 1)

            def normalise(c):
                rows = slice(ST * c, ST * (c + 1))
                y, squares = Y[:, rows, :], SQ[:, rows, :]
                if of_chunk[c]:
                    follow(c)
                step(c, nc.vector.tensor_reduce(MEAN[:, rows], y, AX.X, ALU.add))
                follow(c)
                step(c, nc.vector.scalar_tensor_tensor(out=y, in0=MEAN[:, rows].unsqueeze(2).to_broadcast([P, ST, F]),
                                                       scalar=-1.0 / F, in1=y, op0=ALU.mult, op1=ALU.add))
                follow(c)
                step(c, nc.vector.tensor_tensor(squares, y, y, ALU.mult))
                follow(c)
                step(c, nc.vector.tensor_reduce(RSTD[:, rows], squares, AX.X, ALU.add))
                follow(c)
                nc.vector.tensor_scalar(RSTD[:, rows], RSTD[:, rows], 1.0 / F, EPS, ALU.mult, ALU.add).then_inc(end_var, 1)

            def scaled(l, c):
                rows = slice(ST * c, ST * (c + 1))
                dve.wait_ge(end_rstd, 3 * l + c + 1)
                if l == 0 and c == 0:
                    dve.wait_ge(stored, 16 * B)
                nc.vector.tensor_tensor(X[:, rows, :], Y[:, rows, :], RSTD[:, rows].unsqueeze(2).to_broadcast([P, ST, F]),
                                        ALU.mult).then_inc(end_x, 1)

            def low_part(l, c):
                rows = slice(ST * c, ST * (c + 1))
                dve.wait_ge(end_high, 3 * l + c + 1)
                nc.vector.tensor_tensor(XP[:, rows, F:2 * F], X[:, rows, :], XP[:, rows, 0:F],
                                        ALU.subtract).then_inc(end_low, 1)

            for l in range(4):
                for c in range(NS):
                    if l:
                        add(l - 1, c)
                    else:
                        start(c)
                    normalise(c)
                    if c:
                        scaled(l, c - 1)
                    if c > 1 and l < 3:
                        low_part(l, c - 2)
                scaled(l, NS - 1)
                if l < 3:
                    for c in range(1, NS):
                        low_part(l, c)


_INS = ['x', 'adj', 'L0_gnn_kernel', 'L0_gnn_attention_kernel', 'L0_gnn_attention_kernel_2', 'L0_gnn_bias',
        'L2_gnn_weight', 'L2_gnn_bias']


def kernel(**inputs):
    import numpy as _np
    import concourse.bacc as _bacc
    from concourse import mybir as _mybir
    from concourse.bass_utils import run_bass_kernel_spmd as _run

    nc = _bacc.Bacc("TRN2", target_bir_lowering=False, num_devices=1)
    arrays, args = {}, []
    for name in _INS:
        a = _np.ascontiguousarray(inputs[name])
        arrays[f"in_{name}_dram"] = a
        args.append(nc.dram_tensor(f"in_{name}_dram", a.shape, _mybir.dt.from_np(a.dtype), kind="ExternalInput").ap())
    out = nc.dram_tensor("out_0_dram", (B, N, F), _mybir.dt.float32, kind="ExternalOutput").ap()
    adj_resnorm(nc, *args, out)
    r = _run(nc, [arrays], core_ids=[0])
    return r.results[0]["out_0_dram"]
```
